# Optimizing a Trainium2 kernel written in Bass

```python
import numpy as np
import jax
import jax.numpy as jnp

def _softmax(x, axis=-1):
    return jax.nn.softmax(x, axis=axis)

def _gelu(x):
    return jax.nn.gelu(x, approximate=True)

def _silu(x):
    return jax.nn.silu(x)

def _sigmoid(x):
    return jax.nn.sigmoid(x)

def _layernorm(x, axis=-1, eps=1e-05):
    m = jnp.mean(x, axis=axis, keepdims=True)
    v = jnp.var(x, axis=axis, keepdims=True)
    return (x - m) / jnp.sqrt(v + eps)

def _scatter_add(tgt, idx, src, axis=0):
    return tgt.at[idx].add(src)

def _segment_sum(src, seg, n):
    return jax.ops.segment_sum(src, seg, n)
kernel_name = 'mk_adaln_d1_jaxref_r4_392f64'

def setup_inputs(seed: int=0):
    np.random.seed(seed)
    _w = jnp.asarray

    def _L0_attn_setup():
        import jax, jax.numpy as jnp
        import numpy as np
        B, N, D = (2, 1024, 256)
        H, Dh = (8, 64)
        INNER = H * Dh
        W = 64
        NQ = NKV = 256

        def _forward(x, gamma_h, wq_h, wkv_h, wo_h, ln_g, ln_b, wqkv_l, wo_l, rt_q, rt_kv):
            b, n, d = x.shape
            scale = Dh ** (-0.5)
            neg = -jnp.finfo(x.dtype).max
            mu = jnp.mean(x, -1, keepdims=True)
            var = jnp.var(x, -1, keepdims=True)
            xl = (x - mu) / jnp.sqrt(var + 1e-05) * ln_g + ln_b
            q, k, v = jnp.split(xl @ wqkv_l, 3, -1)

            def heads(t):
                return t.reshape(b, n, H, Dh).transpose(0, 2, 1, 3)
            q, k, v = (heads(q), heads(k), heads(v))
            nw = n // W
            qw = q.reshape(b, H, nw, W, Dh)

            def look_around(t):
                tw = t.reshape(b, H, nw, W, Dh)
                tp = jnp.pad(tw, ((0, 0), (0, 0), (1, 1), (0, 0), (0, 0)))
                return jnp.concatenate([tp[:, :, s:s + nw] for s in range(3)], axis=3)
            kk, vv = (look_around(k), look_around(v))
            wi = jnp.arange(nw)[:, None]
            sh = jnp.arange(3)[None, :]
            valid = (wi + sh - 1 >= 0) & (wi + sh - 1 < nw)
            valid = jnp.repeat(valid, W, axis=1)
            sim = jnp.einsum('bhnid,bhnjd->bhnij', qw * scale, kk)
            sim = jnp.where(valid[None, None, :, None, :], sim, neg)
            attn = jax.nn.softmax(sim, axis=-1)
            lo = jnp.einsum('bhnij,bhnjd->bhnid', attn, vv)
            light_out = lo.reshape(b, H, n, Dh).transpose(0, 2, 1, 3).reshape(b, n, INNER) @ wo_l

            def route(rt, num):
                scores = jnp.einsum('bnd,d->bn', x, rt)
                idx = jnp.argsort(scores, axis=-1)
                s = jnp.take_along_axis(scores, idx, -1)
                s = s - jax.lax.stop_gradient(jnp.max(s, -1, keepdims=True))
                e = jnp.exp(s)
                cs = e / jnp.clip(jnp.cumsum(e, -1), 1e-06, None)
                sel_s, sel_i = (cs[:, -num:], idx[:, -num:])
                sel_s = sel_s + jax.lax.stop_gradient(1.0 - sel_s)
                return (sel_s, sel_i)
            sq, iq = route(rt_q, NQ)
            skv, ikv = route(rt_kv, NKV)
            rq = jnp.take_along_axis(x, iq[:, :, None], 1)
            rkv = jnp.take_along_axis(x, ikv[:, :, None], 1)

            def rms(t):
                t = t / jnp.clip(jnp.linalg.norm(t, axis=-1, keepdims=True), 1e-12, None)
                return t * d ** 0.5 * gamma_h
            hq = (rms(rq) @ wq_h).reshape(b, NQ, H, Dh).transpose(0, 2, 1, 3)
            hk, hv = jnp.split(rms(rkv) @ wkv_h, 2, -1)
            hk = hk.reshape(b, NKV, H, Dh).transpose(0, 2, 1, 3)
            hv = hv.reshape(b, NKV, H, Dh).transpose(0, 2, 1, 3)
            hv = hv * skv[:, None, :, None]
            hsim = jnp.einsum('bhid,bhjd->bhij', hq * scale, hk)
            hattn = jax.nn.softmax(hsim, axis=-1)
            ho = jnp.einsum('bhij,bhjd->bhid', hattn, hv)
            ho = ho.transpose(0, 2, 1, 3).reshape(b, NQ, INNER) @ wo_h
            ho = ho * sq[:, :, None]
            heavy_out = jnp.zeros_like(x).at[jnp.arange(b)[:, None], iq].set(ho)
            return light_out + heavy_out
        key = jax.random.key(seed)
        ks = jax.random.split(key, 8)
        std = 0.02
        return {'x': jax.random.normal(ks[0], (B, N, D), jnp.float32), 'gamma_h': jnp.ones((D,), jnp.float32), 'wq_h': jax.random.normal(ks[1], (D, INNER), jnp.float32) * std, 'wkv_h': jax.random.normal(ks[2], (D, 2 * INNER), jnp.float32) * std, 'wo_h': jax.random.normal(ks[3], (INNER, D), jnp.float32) * std, 'ln_g': jnp.ones((D,), jnp.float32), 'ln_b': jnp.zeros((D,), jnp.float32), 'wqkv_l': jax.random.normal(ks[4], (D, 3 * INNER), jnp.float32) * std, 'wo_l': jax.random.normal(ks[5], (INNER, D), jnp.float32) * std, 'rt_q': jax.random.normal(ks[6], (D,), jnp.float32), 'rt_kv': jax.random.normal(ks[7], (D,), jnp.float32)}
    _L0_attn_in = _L0_attn_setup()

    def _L0_ffn_setup():
        import jax, jax.numpy as jnp
        import numpy as np
        import math
        BETA = 0.9
        THRESHOLD = 1.0
        NUM_STEPS = 5
        ALPHA = 2.0

        @jax.custom_vjp
        def spike_fn(u):
            return (u > 0).astype(u.dtype)

        def _spike_fwd(u):
            return (spike_fn(u), u)

        def _spike_bwd(u, g):
            s = jnp.pi / 2.0 * ALPHA * u
            return (g * (ALPHA / 2.0) / (1.0 + s * s),)
        spike_fn.defvjp(_spike_fwd, _spike_bwd)
        key = jax.random.key(seed)
        k1, k2, k3 = jax.random.split(key, 3)
        n_embd = 256
        x = jax.random.normal(k1, (4, 512, n_embd), dtype=jnp.float32)
        W_fc = jax.random.normal(k2, (4 * n_embd, n_embd), dtype=jnp.float32) / math.sqrt(n_embd)
        W_proj = jax.random.normal(k3, (n_embd, 4 * n_embd), dtype=jnp.float32) / math.sqrt(4 * n_embd)
        return {'x': x, 'W_fc': W_fc, 'W_proj': W_proj}
    _L0_ffn_in = _L0_ffn_setup()
    _L0_c = _w((lambda *s: np.random.randn(*s).astype(np.float32) * 0.05)(8, 256))
    _L0_wmod = _w((lambda *s: np.random.randn(*s).astype(np.float32) * 0.05)(256, 6 * 256) * 256 ** (-0.5))
    _d = {'L0_attn_x': _L0_attn_in['x'], 'L0_attn_gamma_h': _L0_attn_in['gamma_h'], 'L0_attn_wq_h': _L0_attn_in['wq_h'], 'L0_attn_wkv_h': _L0_attn_in['wkv_h'], 'L0_attn_wo_h': _L0_attn_in['wo_h'], 'L0_attn_ln_g': _L0_attn_in['ln_g'], 'L0_attn_ln_b': _L0_attn_in['ln_b'], 'L0_attn_wqkv_l': _L0_attn_in['wqkv_l'], 'L0_attn_wo_l': _L0_attn_in['wo_l'], 'L0_attn_rt_q': _L0_attn_in['rt_q'], 'L0_attn_rt_kv': _L0_attn_in['rt_kv'], 'L0_ffn_W_fc': _L0_ffn_in['W_fc'], 'L0_ffn_W_proj': _L0_ffn_in['W_proj'], 'L0_c': _L0_c, 'L0_wmod': _L0_wmod}
    _x0 = _d['L0_attn_x']
    _d['L0_attn_x'] = jax.random.normal(jax.random.fold_in(jax.random.key(seed), 1), (8, 512, 256), dtype=_x0.dtype)
    del _x0
    return _d

def reference(L0_attn_x, L0_attn_gamma_h, L0_attn_wq_h, L0_attn_wkv_h, L0_attn_wo_h, L0_attn_ln_g, L0_attn_ln_b, L0_attn_wqkv_l, L0_attn_wo_l, L0_attn_rt_q, L0_attn_rt_kv, L0_ffn_W_fc, L0_ffn_W_proj, L0_c, L0_wmod):

    def _L0_attn_ref(x, gamma_h, wq_h, wkv_h, wo_h, ln_g, ln_b, wqkv_l, wo_l, rt_q, rt_kv):
        import jax, jax.numpy as jnp
        import numpy as np
        B, N, D = (2, 1024, 256)
        H, Dh = (8, 64)
        INNER = H * Dh
        W = 64
        NQ = NKV = 256

        def _forward(x, gamma_h, wq_h, wkv_h, wo_h, ln_g, ln_b, wqkv_l, wo_l, rt_q, rt_kv):
            b, n, d = x.shape
            scale = Dh ** (-0.5)
            neg = -jnp.finfo(x.dtype).max
            mu = jnp.mean(x, -1, keepdims=True)
            var = jnp.var(x, -1, keepdims=True)
            xl = (x - mu) / jnp.sqrt(var + 1e-05) * ln_g + ln_b
            q, k, v = jnp.split(xl @ wqkv_l, 3, -1)

            def heads(t):
                return t.reshape(b, n, H, Dh).transpose(0, 2, 1, 3)
            q, k, v = (heads(q), heads(k), heads(v))
            nw = n // W
            qw = q.reshape(b, H, nw, W, Dh)

            def look_around(t):
                tw = t.reshape(b, H, nw, W, Dh)
                tp = jnp.pad(tw, ((0, 0), (0, 0), (1, 1), (0, 0), (0, 0)))
                return jnp.concatenate([tp[:, :, s:s + nw] for s in range(3)], axis=3)
            kk, vv = (look_around(k), look_around(v))
            wi = jnp.arange(nw)[:, None]
            sh = jnp.arange(3)[None, :]
            valid = (wi + sh - 1 >= 0) & (wi + sh - 1 < nw)
            valid = jnp.repeat(valid, W, axis=1)
            sim = jnp.einsum('bhnid,bhnjd->bhnij', qw * scale, kk)
            sim = jnp.where(valid[None, None, :, None, :], sim, neg)
            attn = jax.nn.softmax(sim, axis=-1)
            lo = jnp.einsum('bhnij,bhnjd->bhnid', attn, vv)
            light_out = lo.reshape(b, H, n, Dh).transpose(0, 2, 1, 3).reshape(b, n, INNER) @ wo_l

            def route(rt, num):
                scores = jnp.einsum('bnd,d->bn', x, rt)
                idx = jnp.argsort(scores, axis=-1)
                s = jnp.take_along_axis(scores, idx, -1)
                s = s - jax.lax.stop_gradient(jnp.max(s, -1, keepdims=True))
                e = jnp.exp(s)
                cs = e / jnp.clip(jnp.cumsum(e, -1), 1e-06, None)
                sel_s, sel_i = (cs[:, -num:], idx[:, -num:])
                sel_s = sel_s + jax.lax.stop_gradient(1.0 - sel_s)
                return (sel_s, sel_i)
            sq, iq = route(rt_q, NQ)
            skv, ikv = route(rt_kv, NKV)
            rq = jnp.take_along_axis(x, iq[:, :, None], 1)
            rkv = jnp.take_along_axis(x, ikv[:, :, None], 1)

            def rms(t):
                t = t / jnp.clip(jnp.linalg.norm(t, axis=-1, keepdims=True), 1e-12, None)
                return t * d ** 0.5 * gamma_h
            hq = (rms(rq) @ wq_h).reshape(b, NQ, H, Dh).transpose(0, 2, 1, 3)
            hk, hv = jnp.split(rms(rkv) @ wkv_h, 2, -1)
            hk = hk.reshape(b, NKV, H, Dh).transpose(0, 2, 1, 3)
            hv = hv.reshape(b, NKV, H, Dh).transpose(0, 2, 1, 3)
            hv = hv * skv[:, None, :, None]
            hsim = jnp.einsum('bhid,bhjd->bhij', hq * scale, hk)
            hattn = jax.nn.softmax(hsim, axis=-1)
            ho = jnp.einsum('bhij,bhjd->bhid', hattn, hv)
            ho = ho.transpose(0, 2, 1, 3).reshape(b, NQ, INNER) @ wo_h
            ho = ho * sq[:, :, None]
            heavy_out = jnp.zeros_like(x).at[jnp.arange(b)[:, None], iq].set(ho)
            return light_out + heavy_out
        return _forward(x, gamma_h, wq_h, wkv_h, wo_h, ln_g, ln_b, wqkv_l, wo_l, rt_q, rt_kv)

    def _L0_ffn_ref(x, W_fc, W_proj):
        import jax, jax.numpy as jnp
        import numpy as np
        import math
        BETA = 0.9
        THRESHOLD = 1.0
        NUM_STEPS = 5
        ALPHA = 2.0

        @jax.custom_vjp
        def spike_fn(u):
            return (u > 0).astype(u.dtype)

        def _spike_fwd(u):
            return (spike_fn(u), u)

        def _spike_bwd(u, g):
            s = jnp.pi / 2.0 * ALPHA * u
            return (g * (ALPHA / 2.0) / (1.0 + s * s),)
        spike_fn.defvjp(_spike_fwd, _spike_bwd)
        h = jnp.square(jax.nn.relu(jnp.einsum('bsd,fd->bsf', x, W_fc)))
        y = jnp.einsum('bsf,df->bsd', h, W_proj)

        def step(mem, _):
            reset = jax.lax.stop_gradient(spike_fn(mem - THRESHOLD))
            mem_new = BETA * mem + y - reset * THRESHOLD
            spk = spike_fn(mem_new - THRESHOLD)
            return (mem_new, spk)
        mem0 = jnp.zeros_like(y)
        _, spks = jax.lax.scan(step, mem0, None, length=NUM_STEPS)
        return jnp.sum(spks, axis=0) / NUM_STEPS
    x = L0_attn_x
    mod = (_silu(L0_c) @ L0_wmod).reshape(L0_c.shape[0], 6, 1, -1)
    sa, ca, ga, sb, cb, gb = (mod[:, 0], mod[:, 1], mod[:, 2], mod[:, 3], mod[:, 4], mod[:, 5])
    ga = (2 * (ga >= 0) - 1) * jnp.maximum(jnp.abs(ga), 0.25)
    gb = (2 * (gb >= 0) - 1) * jnp.maximum(jnp.abs(gb), 0.25)
    h = _layernorm(x, axis=-1) * (1 + ca) + sa
    x = x + ga * _L0_attn_ref(h, L0_attn_gamma_h, L0_attn_wq_h, L0_attn_wkv_h, L0_attn_wo_h, L0_attn_ln_g, L0_attn_ln_b, L0_attn_wqkv_l, L0_attn_wo_l, L0_attn_rt_q, L0_attn_rt_kv)
    h = _layernorm(x, axis=-1) * (1 + cb) + sb
    x = x + gb * _L0_ffn_ref(h, L0_ffn_W_fc, L0_ffn_W_proj)
    return x

_drawn_inputs = setup_inputs


def setup_inputs(seed=0):
    import zlib

    import numpy as np

    out = dict(_drawn_inputs(seed))
    spreads = {'L0_attn_gamma_h': (1.0, 0.6), 'L0_attn_ln_g': (1.0, 0.6), 'L0_attn_ln_b': (0.0, 0.8)}
    factors = {'L0_attn_wq_h': 8.0,
     'L0_attn_wkv_h': 8.0,
     'L0_attn_wo_h': 8.0,
     'L0_attn_wqkv_l': 8.0,
     'L0_attn_wo_l': 8.0,
     'L0_attn_rt_q': 8.0,
     'L0_attn_rt_kv': 8.0}
    for name, (base, spread) in spreads.items():
        noise = np.random.default_rng([zlib.crc32(name.encode()), seed]).standard_normal(out[name].shape)
        drawn = base * np.exp(spread * noise) if base else spread * noise
        out[name] = jnp.asarray(drawn.astype(out[name].dtype))
    for name, factor in factors.items():
        out[name] = (out[name] * factor).astype(out[name].dtype)
    return out
```

```python
from contextlib import ExitStack

import concourse.bass as bass
from concourse import mybir

F32 = mybir.dt.float32
F32R = mybir.dt.float32r
BF16 = mybir.dt.bfloat16
I32 = mybir.dt.int32
ALU = mybir.AluOpType
ACT = mybir.ActivationFunctionType
AX = mybir.AxisListType

P = 128
B, N, D = 8, 512, 256
H, DH = 8, 64
INNER = H * DH
W = 64
SEL = 256
F = 4 * D
STEPS = 5
T = N // P
KD = D // P
PAIRS = H // 2
NW = N // W
FT = F // P
LIGHT = PAIRS * T
HEAVY = PAIRS * (SEL // P)
SLOTS = LIGHT + HEAVY
SCALE = DH ** -0.5
BANKS = 4

PRE, POST = -1, SLOTS
SLOT_UNITS = {
    PRE: [("Q", 0), ("K", 0), ("V", 0)],
    0: [("V", 1)], 1: [("V", 2), ("Q", 1)], 2: [("V", 3), ("K", 1)], 3: [("Q", 2)], 4: [("K", 2)],
    5: [("Z3", 0), ("Z3", 1)], 6: [("FC", 0), ("FC", 1)], 7: [("FC", 2), ("Q", 3)],
    8: [("FC", 3)], 9: [("FC", 4)], 10: [("K", 3), ("FC", 5)],
    11: [("FC", 6), ("SR", 0)], 12: [("FC", 7), ("HT", 0)],
    13: [("HT", 1), ("HQ", 0), ("RK", 0), ("SR", 1)], 14: [("HK", 0), ("Y", 0)], 15: [("Y", 1), ("RK", 1)], 16: [("HV", 0), ("HV", 1)],
    17: [("Y", 2), ("ZT", 0)], 18: [("HQ", 1), ("HK", 1)], 19: [("LO", 0), ("ZT", 1)],
    20: [("LO", 1), ("Y", 3)], 21: [("LO", 2)], 22: [("LO", 3)], 23: [],
    POST: [("HO", 0), ("HO", 1)],
}
MLP_UNITS = ("Z3", "FC", "Y")
NEXT_UNITS = ("ZT", "SR", "RK")


def slot_units(slot, first, last):
    return [u for u in SLOT_UNITS[slot]
            if not (first and u[0] in MLP_UNITS) and not (last and u[0] in NEXT_UNITS)]


def iteration_units(first, last):
    return [u for s in range(PRE, POST + 1) for u in slot_units(s, first, last)]


SEGMENTS = {
    "setup": [("SC", 0), ("MC", 0)] + [("MR", i) for i in range(3)]
             + [("WF", i) for i in range(4)] + [("WP", i) for i in range(4)],
    "start": [("ZT", 0), ("ZT", 1), ("SR", 0), ("RK", 0), ("SR", 1), ("RK", 1)],
    "first": iteration_units(True, False),
    "loop": iteration_units(False, False),
    "last": iteration_units(False, True),
    "tail": [("Z3", 0), ("Z3", 1)] + [("FC", f) for f in range(FT)] + [("Y", t) for t in range(T)],
}
USES = {s: [len(u[k::BANKS]) for k in range(BANKS)] for s, u in SEGMENTS.items()}


def bank_use(segment, b, unit):
    i = SEGMENTS[segment].index(unit)
    bank, before = i % BANKS, i // BANKS
    for s in SEGMENTS:
        if s == segment:
            break
        before += USES[s][bank] * (B - 2 if s == "loop" else 1)
    if segment == "loop":
        return bank, b * USES["loop"][bank] + (before - USES["loop"][bank])
    return bank, before


def score_columns(s):
    if s >= LIGHT:
        return (0, SEL), (SEL, 2 * SEL)
    m = s % T
    return (0, P if m == T - 1 else P + W), (2 * P if m == 0 else P + W, 3 * P)


def adaln_block_kernel(nc, x, gamma_h, wq_h, wkv_h, wo_h, ln_g, ln_b, wqkv_l, wo_l, rt_q, rt_kv,
                       w_fc, w_proj, c, wmod, out):
    with ExitStack() as ctx:
        def sb(name, shape, dt=F32):
            return ctx.enter_context(nc.sbuf_tensor(name, shape, dt))

        def sem(name):
            return ctx.enter_context(nc.semaphore(name))

        mod_rows = nc.dram_tensor("mod_rows", [B, 4 * D], F32, kind="Internal").ap()
        sorted_rows = [nc.dram_tensor(f"sorted_rows{r}", [N, D], F32, kind="Internal").ap() for r in range(2)]
        routed_out = nc.dram_tensor("routed_out", [N, D], F32, kind="Internal").ap()

        ident = sb("ident", [P, P])
        ones = sb("ones", [P, P])
        ones_bf = sb("ones_bf", [P, 2], BF16)
        later = sb("later", [P, P], BF16)
        neg_half = sb("neg_half", [P, T])
        router = sb("router", [P, 2, D])
        ln_cols = sb("ln_cols", [P, 2, KD])
        gamma_cols = sb("gamma_cols", [P, 2, KD])
        shift_b = sb("shift_b", [P, KD, B])
        scale_b = sb("scale_b", [P, KD, B])
        wqkv = [sb(f"wqkv{i}", [P, KD, 3 * INNER], F32R) for i in range(2)]
        wq_r = [sb(f"wq_r{i}", [P, KD, INNER], F32R) for i in range(2)]
        wkv_r = [sb(f"wkv_r{i}", [P, KD, 2 * INNER], F32R) for i in range(2)]
        wfcT = [sb(f"wfcT{i}", [P, KD, F], F32R) for i in range(2)]
        wprojT = sb("wprojT", [P, FT, D])
        wo_light = sb("wo_light", [P, PAIRS, D])
        wo_heavy = sb("wo_heavy", [P, PAIRS, D])

        xa = sb("xa", [P, T, D])
        mod_a = sb("mod_a", [P, 2, D])
        h1 = sb("h1", [P, T, D])
        hn = sb("hn", [P, T, D])
        bn6 = sb("bn6", [P, 3, T, 6])
        mv = sb("mv", [P, 3, T, 2])
        veps = sb("veps", [P, 4, T])
        rstd = sb("rstd", [P, 4, T])
        musq = sb("musq", [P, T])
        score = sb("score", [P, 2, T])
        marks = sb("marks", [P, 4])
        full = sb("full", [P, 2, N])
        xT = [sb(f"xT{i}", [P, KD, N], F32R) for i in range(2)]
        rank = sb("rank", [P, 2, T], I32)
        rank_kept = sb("rank_kept", [P, T], I32)
        late = sb("late", [P, 2304])
        diag = late[:, 0:512].rearrange("p (t n) -> p t n", t=T)
        score_row = late[:, 512:1024]
        greater = late[:, 1024:2048].bitcast(BF16).rearrange("p (t n) -> p t n", t=T)
        products = late[:, 1024:2048].bitcast(BF16).rearrange("p (r t n) -> p r t n", r=2, t=T)
        tie = late[:, 2048:2304].bitcast(BF16).rearrange("p (t n) -> p t n", t=T)

        qbd = sb("qbd", [P, 2, NW, P])
        kT = sb("kT", [P, 2, N])
        v = sb("v", [P, T, INNER])
        probs = sb("probs", [P, 2, 512])
        probsT = sb("probsT", [P, 512])
        row_min = sb("row_min", [P, 2, 2])
        row_sum = sb("row_sum", [P, 2, 2])
        row_inv = sb("row_inv", [P, 2, 2])
        loT = sb("loT", [P, PAIRS, N])
        routed = sb("routed", [P, 2, 2, D])
        qbd_r = qbd[:, :, :, :].rearrange("p a (c w) q -> p (a c) w q", c=2)
        kT_r = kT[:, :, :].rearrange("p a (c n) -> p (a c) n", c=2)
        v_r = v[:, 0:2, :]
        hoT = late[:, 0:1024].rearrange("p (t n) -> p t n", t=PAIRS)
        ho = late[:, 1024:1536].rearrange("p (t n) -> p t n", t=2)

        gate_a = sb("gate_a", [P, D])
        gate_b = sb("gate_b", [P, D])
        lg = sb("lg", [P, 2, D])
        lx = sb("lx", [P, T, D])
        gathered = hn
        x2 = sb("x2", [P, T, D])
        h2T = [sb(f"h2T{i}", [P, KD, N], F32R) for i in range(2)]
        hT = [a[:, :, :].rearrange("p k n -> p (k n)").rearrange("p (r k n) -> p r k n", r=2, k=KD)
              for a in h2T]
        hid = sb("hid", [P, FT, N])
        y = sb("y", [P, T, D])
        drive = sb("drive", [P, 2 * D])
        neg_mem = sb("neg_mem", [P, 2 * D])
        spikes = sb("spikes", [P, 2, 2 * D])

        raw_wmod = [v[:, 0:3, :].rearrange("p t n -> p (t n)"), loT[:, 0:3, :].rearrange("p t n -> p (t n)")]
        raw_wqkv = hid[:, 0:6, :].rearrange("p t n -> p (t n)").rearrange("p (k n) -> p k n", k=KD)
        raw_wq = routed[:, :, :, :].rearrange("p a b n -> p (a b n)").rearrange("p (k n) -> p k n", k=KD)
        raw_wkv = [full[:, :, :].rearrange("p a n -> p (a n)"), spikes[:, :, :].rearrange("p a n -> p (a n)")]
        raw_wfc = [y, x2]
        raw_wproj = [kT[:, :, :].rearrange("p a n -> p (a n)"), lx[:, :, :].rearrange("p a n -> p (a n)")]
        silu = hn[0:B, 0:3, :]
        siluT = sb("siluT", [P, KD, B])
        mod_norm = v[0:B, 3, :]
        mod_gate = loT[0:B, 3, :]
        gates = drive[0:B, :]
        gates_abs = neg_mem[0:B, :]
        gates_sign = lg[0:B, :, :].rearrange("b a d -> b (a d)")

        ps_scores = [ctx.enter_context(nc.psum_tensor(f"ps_scores{i}", [P, 512], F32)) for i in range(2)]
        ps_pT = ctx.enter_context(nc.psum_tensor("ps_pT", [P, 512], F32))
        ps_oT = ctx.enter_context(nc.psum_tensor("ps_oT", [P, 512], F32))
        ps_unit = [ctx.enter_context(nc.psum_tensor(f"ps_unit{i}", [P, 512], F32)) for i in range(BANKS)]

        filled = [sem(f"filled{i}") for i in range(BANKS)]
        drained = [sem(f"drained{i}") for i in range(BANKS)]
        consts_made = sem("consts_made")
        zeros_made = sem("zeros_made")
        zero_rows_stored = sem("zero_rows_stored")
        x_loaded = sem("x_loaded")
        mod_a_loaded = sem("mod_a_loaded")
        small_loaded = sem("small_loaded")
        c_loaded = sem("c_loaded")
        wmod_loaded = sem("wmod_loaded")
        wqkv_loaded = sem("wqkv_loaded")
        wr_loaded = sem("wr_loaded")
        wmlp_loaded = sem("wmlp_loaded")
        wo_loaded = sem("wo_loaded")
        exp_c = sem("exp_c")
        setup_chain = sem("setup_chain")
        silu_ready = sem("silu_ready")
        mod_stored = sem("mod_stored")
        mod_ready = sem("mod_ready")
        high_made = sem("high_made")
        low_made = sem("low_made")
        wfull = sem("wfull")
        scores_ready = sem("scores_ready")
        min_ready = sem("min_ready")
        exp_ready = sem("exp_ready")
        inv_ready = sem("inv_ready")
        probs_ready = sem("probs_ready")
        pT_ready = sem("pT_ready")
        pT_copied = sem("pT_copied")
        outer_done = sem("outer_done")
        oT_ready = sem("oT_ready")
        oT_copied = sem("oT_copied")
        ln_chain = sem("ln_chain")
        mv1_ready = sem("mv1_ready")
        mv2_ready = sem("mv2_ready")
        mv3_ready = sem("mv3_ready")
        pool_chain = sem("pool_chain")
        norm_ready = sem("norm_ready")
        pool_chain3 = sem("pool_chain3")
        rstd1_ready = sem("rstd1_ready")
        rstd2_ready = sem("rstd2_ready")
        rstd3_ready = sem("rstd3_ready")
        h1_ready = sem("h1_ready")
        hn_ready = sem("hn_ready")
        score_ready = sem("score_ready")
        z_ready = sem("z_ready")
        xT_high = sem("xT_high")
        xT_low = sem("xT_low")
        diag_ready = sem("diag_ready")
        compared = sem("compared")
        scattered = sem("scattered")
        sorted_loaded = sem("sorted_loaded")
        rank_saved = sem("rank_saved")
        hT_high = sem("hT_high")
        lx_loaded = sem("lx_loaded")
        gate_a_loaded = sem("gate_a_loaded")
        gate_b_loaded = sem("gate_b_loaded")
        lx_ready = sem("lx_ready")
        ho_stored = sem("ho_stored")
        rows_gathered = sem("rows_gathered")
        x2_ready = sem("x2_ready")
        d_chain = sem("d_chain")
        z3_ready = sem("z3_ready")
        h2_high = sem("h2_high")
        h2_low = sem("h2_low")
        hid_ready = sem("hid_ready")
        lif_chain = sem("lif_chain")
        y_free = sem("y_free")
        out_chain = sem("out_chain")
        final_ready = sem("final_ready")
        waits_passed = sem("waits_passed")
        out_stored = sem("out_stored")

        def wait_drained(eng, segment, b, unit):
            bank, before = bank_use(segment, b, unit)
            eng.wait_ge(drained[bank], before + 1)

        def seal_waits(eng):
            eng.sem_inc(waits_passed, 1)

        block = ctx.enter_context(nc.Block())

        @block.sync
        def _(sp):
            sp.dma_start(silu[:, 0, :], c).then_inc(c_loaded, 16)
            for k in range(KD):
                sp.dma_start(raw_wmod[k], wmod[k * P:(k + 1) * P, :]).then_inc(wmod_loaded, 16)
            sp.dma_start(xa[:, :, :], x[0].rearrange("(t p) d -> p t d", p=P)).then_inc(x_loaded, 16)
            for i, a in enumerate((rt_q, rt_kv)):
                sp.dma_start(router[:, i, :], a.partition_broadcast(P)).then_inc(small_loaded, 16)
            sp.dma_start(raw_wqkv, wqkv_l.rearrange("(k p) n -> p k n", p=P)).then_inc(wqkv_loaded, 16)
            sp.dma_start(raw_wq, wq_h.rearrange("(k p) n -> p k n", p=P)).then_inc(wr_loaded, 16)
            for k in range(KD):
                sp.dma_start(raw_wkv[k], wkv_h[k * P:(k + 1) * P, :]).then_inc(wr_loaded, 16)
            for i in range(2):
                sp.dma_start(raw_wfc[i][:, :, :],
                             w_fc[i * 512:(i + 1) * 512, :].rearrange("(t p) d -> p t d", p=P)
                             ).then_inc(wmlp_loaded, 16)
                sp.dma_start(raw_wproj[i], w_proj[i * P:(i + 1) * P, :]).then_inc(wmlp_loaded, 16)
            sp.dma_start(wo_light[:, :, :], wo_l.rearrange("(t p) n -> p t n", p=P)).then_inc(wo_loaded, 16)
            sp.dma_start(wo_heavy[:, :, :], wo_h.rearrange("(t p) n -> p t n", p=P)).then_inc(wo_loaded, 16)
            sp.wait_ge(zeros_made, 2)
            sp.dma_start(routed_out[0:SEL, :].rearrange("(p r) d -> p (r d)", p=P),
                         probs[:, 0, :]).then_inc(zero_rows_stored, 16)
            sp.wait_ge(mod_ready, 1)
            sp.dma_start(mod_rows[:, 0:2 * D], mod_norm).then_inc(mod_stored, 16)
            sp.dma_start(mod_rows[:, 2 * D:4 * D], mod_gate).then_inc(mod_stored, 16)
            sp.wait_ge(mod_stored, 32)

            def mod_row(n, first, last):
                row = mod_rows[n:n + 1, first * D:last * D] if isinstance(n, int) else \
                    mod_rows[bass.ds(n, 1), first * D:last * D]
                return row.rearrange("a n -> (a n)").partition_broadcast(P)

            def batch(t, n):
                a = t[n:n + 1] if isinstance(n, int) else t[bass.ds(n, 1)]
                return a.rearrange("a (t p) d -> p (a t) d", p=P)

            def load_sorted(n):
                sp.wait_ge(scattered, 128 * n + 128)
                for r in range(2):
                    sp.dma_start(routed[:, r, :, :], sorted_rows[r][N - SEL:N, :].rearrange(
                        "(t p) d -> p t d", p=P)).then_inc(sorted_loaded, 16)

            def store(n, half):
                sp.wait_ge(final_ready, 2 * n + half + 2)
                sp.dma_start(batch(out, n)[:, 2 * half:2 * half + 2, :],
                             spikes[:, half, :].rearrange("p (t d) -> p t d", t=2)).then_inc(out_stored, 16)

            def iteration(segment, b, first=False, last=False):
                if not first:
                    sp.wait_ge(ho_stored, 16 * b)
                sp.dma_start(gate_a[:, :], mod_row(b, 2, 3)).then_inc(gate_a_loaded, 16)
                if not last:
                    sp.wait_ge(xT_high, 2 * b + 2)
                    sp.dma_start(xa[:, :, :], batch(x, b + 1)).then_inc(x_loaded, 16)
                    sp.wait_ge(h1_ready, b + 1)
                    sp.dma_start(mod_a[:, :, :].rearrange("p a d -> p (a d)"),
                                 mod_row(b + 1, 0, 2)).then_inc(mod_a_loaded, 16)
                if not first:
                    sp.wait_ge(final_ready, 2 * b - 1)
                    sp.dma_start(gate_b[:, :], mod_row(b - 1, 3, 4)).then_inc(gate_b_loaded, 16)
                    sp.wait_ge(x2_ready, b)
                sp.dma_start(lx[:, :, :], batch(x, b)).then_inc(lx_loaded, 16)
                if not last:
                    wait_drained(sp, segment, b, ("HT", 1))
                    load_sorted(b + 1)
                if not first:
                    store(b - 1, 0)
                    sp.wait_ge(rows_gathered, 64 * b)
                    seal_waits(sp)
                for t in range(2):
                    wait_drained(sp, segment, b, ("HO", t))
                    seal_waits(sp)
                sp.dma_start(routed_out[N - SEL:N, :].rearrange("(t p) d -> p t d", p=P),
                             ho).then_inc(ho_stored, 16)
                if not first:
                    store(b - 1, 1)

            sp.dma_start(mod_a[:, :, :].rearrange("p a d -> p (a d)"), mod_row(0, 0, 2)).then_inc(mod_a_loaded, 16)
            load_sorted(0)
            wait_drained(sp, "setup", 0, ("WP", 3))
            iteration("first", 0, first=True)
            with sp.Fori(1, B - 1) as b:
                iteration("loop", b)
            iteration("last", B - 1, last=True)
            sp.wait_ge(final_ready, 2 * B - 1)
            sp.dma_start(gate_b[:, :], mod_row(B - 1, 3, 4)).then_inc(gate_b_loaded, 16)
            store(B - 1, 0)
            store(B - 1, 1)
            sp.wait_ge(out_stored, 32 * B + 16)

        @block.gpsimd
        def _(pool):
            pool.memset(ident[:, :], 0.0).then_inc(consts_made, 1)
            pool.memset(later[:, :], 1.0).then_inc(consts_made, 1)
            pool.memset(ones[:, :], 1.0).then_inc(consts_made, 1)
            pool.memset(ones_bf[:, :], 1.0).then_inc(consts_made, 1)
            pool.memset(neg_half[:, :], -0.5).then_inc(consts_made, 1)
            pool.wait_ge(consts_made, 2)
            pool.affine_select(out=ident[:, :], in_=ident[:, :], compare_op=ALU.not_equal, fill=1.0, base=0,
                               pattern=[[-1, P]], channel_multiplier=1).then_inc(consts_made, 1)
            pool.affine_select(out=later[:, :], in_=later[:, :], compare_op=ALU.is_gt, fill=0.0, base=0,
                               pattern=[[1, P]], channel_multiplier=-1).then_inc(consts_made, 1)
            pool.memset(veps[:, :, :], 1.0).then_inc(final_ready, 1)
            pool.wait_ge(consts_made, 7)
            pool.wait_ge(final_ready, 1)

            def rstd_of(i, chain, count):
                pool.tensor_scalar(veps[:, i, :], mv[:, i, :, 1], 1e-5, 1.0, ALU.add, ALU.mult).then_inc(chain, 1)
                pool.wait_ge(chain, count)
                return pool.tensor_tensor(rstd[:, i, :], veps[:, i, :], neg_half[:, :], ALU.pow)

            def rstd1(n):
                pool.wait_ge(mv1_ready, n + 1)
                seal_waits(pool)
                rstd_of(0, pool_chain, 5 * n + 1).then_inc(rstd1_ready, 1)

            def rstd2(n):
                pool.wait_ge(mv2_ready, n + 1)
                seal_waits(pool)
                rstd_of(1, pool_chain, 5 * n + 2).then_inc(rstd2_ready, 1)
                pool.tensor_tensor(musq[:, :], mv[:, 1, :, 0], mv[:, 1, :, 0], ALU.mult).then_inc(pool_chain, 1)
                pool.wait_ge(pool_chain, 5 * n + 3)
                pool.tensor_tensor(musq[:, :], musq[:, :], mv[:, 1, :, 1], ALU.add).then_inc(pool_chain, 1)
                pool.wait_ge(pool_chain, 5 * n + 4)
                seal_waits(pool)
                pool.tensor_scalar(veps[:, 3, :], musq[:, :], float(D), 1e-24, ALU.mult, ALU.max).then_inc(pool_chain, 1)
                pool.wait_ge(pool_chain, 5 * n + 5)
                pool.tensor_tensor(rstd[:, 3, :], veps[:, 3, :], neg_half[:, :], ALU.pow).then_inc(norm_ready, 1)

            def norm_rows(n):
                pool.wait_ge(h1_ready, n + 1)
                pool.wait_ge(norm_ready, n + 1)
                seal_waits(pool)
                for t in range(T):
                    ins = pool.tensor_scalar(hn[:, t, :], h1[:, t, :], rstd[:, 3, t:t + 1], 1.0, ALU.mult, ALU.mult)
                ins.then_inc(hn_ready, 1)

            def score_diag(segment, n, r):
                pool.wait_ge(score_ready, n + 1)
                if r == 1:
                    wait_drained(pool, segment, n - 1, ("SR", 0))
                seal_waits(pool)
                for t in range(T):
                    ins = pool.tensor_scalar(diag[:, t, :], ident[:, :], score[:, r, t:t + 1], 1.0, ALU.mult, ALU.mult)
                ins.then_inc(diag_ready, 1)

            def scatter(segment, n, r):
                wait_drained(pool, segment, n - 1, ("RK", r))
                pool.wait_ge(hn_ready, n + 1)
                if not (isinstance(n, int) and n == 0):
                    pool.wait_ge(sorted_loaded, 32 * n)
                seal_waits(pool)
                for t in range(T):
                    pool.indirect_dma_start(out=sorted_rows[r], out_offset=bass.IndirectOffsetOnAxis(
                        ap=rank[:, r, t:t + 1], axis=0), in_=hn[:, t, :], in_offset=None).then_inc(scattered, 16)

            def save_rank(segment, n):
                if not (isinstance(n, int) and n == 0):
                    pool.wait_ge(rows_gathered, 64 * n)
                wait_drained(pool, segment, n - 1, ("RK", 0))
                seal_waits(pool)
                pool.tensor_copy(rank_kept[:, :], rank[:, 0, :]).then_inc(rank_saved, 1)

            def gather(b, last):
                pool.wait_ge(rank_saved, b + 1)
                pool.wait_ge(ho_stored, 16 * b + 16)
                if not last:
                    pool.wait_ge(scattered, 128 * b + 256)
                seal_waits(pool)
                for t in range(T):
                    pool.indirect_dma_start(out=gathered[:, t, :], out_offset=None, in_=routed_out,
                                            in_offset=bass.IndirectOffsetOnAxis(ap=rank_kept[:, t:t + 1], axis=0)
                                            ).then_inc(rows_gathered, 16)

            def rstd3(n):
                pool.wait_ge(mv3_ready, n + 1)
                seal_waits(pool)
                rstd_of(2, pool_chain3, n + 1).then_inc(rstd3_ready, 1)

            def low_part(segment, b, unit):
                kind, k = unit
                n, highs, lows, parts = (b + 1, xT_high, xT_low, xT) if kind == "ZT" else \
                    (b - 1, h2_high, h2_low, h2T)
                wait_drained(pool, segment, b, unit)
                pool.wait_ge(highs, 2 * n + k + 1)
                pool.tensor_tensor(parts[1][:, k, :], full[:, k, :], parts[0][:, k, :].bitcast(F32),
                                   ALU.subtract).then_inc(lows, 1)

            def square(segment, b, f):
                wait_drained(pool, segment, b, ("FC", f))
                pool.tensor_tensor(hid[:, f, :], hid[:, f, :], hid[:, f, :], ALU.mult).then_inc(hid_ready, 1)

            def add_x(segment, b, t):
                pool.wait_ge(lx_loaded, 16 * b + 16)
                wait_drained(pool, segment, b, ("LO", t))
                pool.tensor_tensor(lx[:, t, :], lx[:, t, :], lg[:, t % 2, :], ALU.add).then_inc(lx_ready, 1)

            def final(n, half):
                sp2 = spikes[:, half, :].rearrange("p (t d) -> p t d", t=2)
                pool.wait_ge(gate_b_loaded, 16 * n + 16)
                pool.wait_ge(y_free, 2 * n + half + 3)
                pool.tensor_tensor(sp2, sp2, gate_b[:, :].unsqueeze(1).to_broadcast([P, 2, D]),
                                   ALU.mult).then_inc(out_chain, 1)
                pool.wait_ge(out_chain, 2 * n + half + 1)
                pool.tensor_tensor(sp2, sp2, x2[:, 2 * half:2 * half + 2, :], ALU.add).then_inc(final_ready, 1)

            def unit(segment, b, u):
                kind, i = u
                if kind == "FC":
                    square(segment, b, i)
                elif kind in ("Z3", "ZT"):
                    low_part(segment, b, u)
                elif kind == "LO":
                    add_x(segment, b, i)

            def iteration(segment, b, first=False, last=False):
                for s in range(PRE, POST + 1):
                    for u in slot_units(s, first, last):
                        unit(segment, b, u)
                    if not first:
                        if s == 3:
                            rstd3(b - 1)
                        if s == 20:
                            final(b - 1, 0)
                    if not last:
                        if s == 4:
                            rstd1(b + 1)
                        if s == 8:
                            rstd2(b + 1)
                            norm_rows(b + 1)
                        if s == 9:
                            score_diag(segment, b + 1, 0)
                        if s == 12:
                            score_diag(segment, b + 1, 1)
                        if s == 14:
                            scatter(segment, b + 1, 0)
                        if s == 16:
                            scatter(segment, b + 1, 1)
                gather(b, last)
                if not first:
                    final(b - 1, 1)
                if not last:
                    save_rank(segment, b + 1)

            rstd1(0)
            rstd2(0)
            norm_rows(0)
            for k in range(KD):
                low_part("start", -1, ("ZT", k))
            for r in range(2):
                score_diag("start", 0, r)
                scatter("start", 0, r)
            save_rank("start", 0)
            iteration("first", 0, first=True)
            with pool.Fori(1, B - 1) as b:
                iteration("loop", b)
            iteration("last", B - 1, last=True)
            rstd3(B - 1)
            for u in SEGMENTS["tail"]:
                unit("tail", B, u)
            final(B - 1, 0)
            final(B - 1, 1)

        @block.scalar
        def _(act):
            act.dma_start(ln_cols[:, 0, :], ln_g.rearrange("(k p) -> p k", p=P), allow_slow_non_contiguous=True).then_inc(small_loaded, 16)
            act.dma_start(ln_cols[:, 1, :], ln_b.rearrange("(k p) -> p k", p=P), allow_slow_non_contiguous=True).then_inc(small_loaded, 16)
            act.dma_start(gamma_cols[:, 0, :], gamma_h.rearrange("(k p) -> p k", p=P), allow_slow_non_contiguous=True).then_inc(small_loaded, 16)
            act.wait_ge(c_loaded, 16)
            act.activation(silu[:, 1, :], silu[:, 0, :], ACT.Exp, scale=-1.0).then_inc(exp_c, 1)
            act.wait_ge(wqkv_loaded, 16)
            for k in range(KD):
                act.activation(wqkv[0][:, k, :], raw_wqkv[:, k, :], ACT.Copy).then_inc(high_made, 1)

            def drain(segment, b, unit):
                bank, before = bank_use(segment, b, unit)
                act.wait_ge(filled[bank], before + 1)
                return ps_unit[bank], drained[bank]

            def query(segment, b, unit):
                kind, i = unit
                ps, free = drain(segment, b, unit)
                for h in range(2):
                    rows = slice(h * DH, (h + 1) * DH)
                    if kind == "Q":
                        src = ps[rows, :].rearrange("p (w q) -> p w q", q=W)
                        dst = qbd[rows, i % 2, :, h * W:(h + 1) * W]
                    else:
                        src = ps[rows, :].rearrange("p (a w q) -> p a w q", a=2, q=W)
                        dst = qbd_r[rows, 2 * i:2 * i + 2, :, h * W:(h + 1) * W]
                    ins = act.activation(dst, src, ACT.Copy, scale=-SCALE)
                ins.then_inc(free, 1)

            def unit(segment, b, u):
                kind, i = u
                if kind in ("Q", "HQ"):
                    query(segment, b, u)
                elif kind == "ZT":
                    ps, free = drain(segment, b, u)
                    if segment == "start":
                        act.wait_ge(small_loaded, 80)
                        act.wait_ge(low_made, 6)
                    else:
                        act.wait_ge(xT_low, 2 * b + 2)
                    if segment in ("loop", "last"):
                        act.wait_ge(h2_low, 2 * b)
                    act.activation(full[:, i, :], ps[:, :], ACT.Identity, bias=ln_cols[:, 1, i:i + 1],
                                   scale=ln_cols[:, 0, i:i + 1]).then_inc(free, 1)
                elif kind == "Z3":
                    ps, free = drain(segment, b, u)
                    n = b - 1
                    act.wait_ge(xT_low, 2 * B if segment == "tail" else 2 * b + 2)
                    col = slice(n, n + 1) if isinstance(n, int) else bass.ds(n, 1)
                    act.activation(full[:, i, :], ps[:, :], ACT.Identity, bias=shift_b[:, i, col],
                                   scale=scale_b[:, i, col]).then_inc(free, 1)
                elif kind == "SR":
                    ps, free = drain(segment, b, u)
                    if i == 1 or segment != "start":
                        act.wait_ge(compared, 2 * b + 2 + i)
                    act.activation(score_row, ps[:, :], ACT.Copy).then_inc(free, 1)
                elif kind == "HT":
                    ps, _ = drain(segment, b, u)
                    for k in range(KD):
                        ins = act.activation(hT[0][:, i, k, :], ps[:, k * SEL:(k + 1) * SEL], ACT.Identity,
                                             scale=gamma_cols[:, 1, k:k + 1])
                    ins.then_inc(hT_high, 1)
                elif kind == "FC":
                    ps, free = drain(segment, b, u)
                    act.activation(hid[:, i, :], ps[:, :], ACT.Relu).then_inc(free, 1)
                elif kind == "Y":
                    ps, free = drain(segment, b, u)
                    act.wait_ge(y_free, 2 * b - 1 + i // 2)
                    act.activation(y[:, i, :], ps[:, 0:D], ACT.Copy).then_inc(free, 1)

            def exp_step(b, s):
                act.wait_ge(min_ready, SLOTS * b + s + 1)
                if isinstance(b, int) and b == 0 and s == 0:
                    act.wait_ge(zero_rows_stored, 16)
                ps = ps_scores[s % 2]
                for half, (lo, hi) in enumerate(score_columns(s)):
                    ins = act.activation(probs[:, s % 2, lo:hi], ps[:, lo:hi], ACT.Exp,
                                         bias=row_min[:, s % 2, half:half + 1], scale=-1.0,
                                         accum_out=row_sum[:, s % 2, half:half + 1])
                ins.then_inc(exp_ready, 1)

            def copy_pT(b, s):
                act.wait_ge(pT_ready, SLOTS * b + s + 1)
                n = 384 if s < LIGHT else 512
                act.activation(probsT[:, 0:n], ps_pT[:, 0:n], ACT.Copy).then_inc(pT_copied, 1)

            def iteration(segment, b, first=False, last=False):
                for u in slot_units(PRE, first, last):
                    unit(segment, b, u)
                exp_step(b, 0)
                for s in range(SLOTS):
                    if s > 0:
                        copy_pT(b, s - 1)
                    if s + 1 < SLOTS:
                        exp_step(b, s + 1)
                    for u in slot_units(s, first, last):
                        unit(segment, b, u)
                copy_pT(b, SLOTS - 1)
                for u in slot_units(POST, first, last):
                    unit(segment, b, u)

            act.wait_ge(wr_loaded, 48)
            for k in range(KD):
                act.activation(wq_r[0][:, k, :], raw_wq[:, k, :], ACT.Copy).then_inc(high_made, 1)
                act.activation(wkv_r[0][:, k, :], raw_wkv[k], ACT.Copy).then_inc(high_made, 1)
            for i in range(4):
                ps, free = drain("setup", 0, ("WF", i))
                act.activation(wfcT[0][:, i // 2, (i % 2) * 512:(i % 2 + 1) * 512], ps[:, :],
                               ACT.Copy).then_inc(high_made, 1)
            for i in range(4):
                ps, free = drain("setup", 0, ("WP", i))
                act.activation(wprojT[:, 2 * i:2 * i + 2, :].rearrange("p a n -> p (a n)"), ps[:, :],
                               ACT.Copy).then_inc(free, 1)
            for u in SEGMENTS["start"]:
                unit("start", -1, u)
            iteration("first", 0, first=True)
            with act.Fori(1, B - 1) as b:
                iteration("loop", b)
            iteration("last", B - 1, last=True)
            for u in SEGMENTS["tail"]:
                unit("tail", B, u)

        @block.tensor
        def _(pe):
            def fill(segment, b, unit):
                bank, before = bank_use(segment, b, unit)
                if not (isinstance(before, int) and before == 0):
                    pe.wait_ge(drained[bank], before)
                return ps_unit[bank], filled[bank]

            def split_product(ps, w, w_cols, a, a_cols):
                n = 0
                for k in range(KD):
                    for wi, ai in ((0, 0), (0, 1), (1, 0)):
                        ins = pe.matmul(ps, w(wi, k, w_cols), a(ai, k, a_cols), start=(n == 0), stop=(n == 3 * KD - 1))
                        n += 1
                return ins

            def unit(segment, b, u):
                kind, i = u
                ps, full_bank = fill(segment, b, u)
                if kind in ("Q", "K"):
                    if i == 0 and kind == "Q":
                        pe.wait_ge(xT_high, 2 * b + 2)
                        pe.wait_ge(xT_low, 2 * b + 2)
                    c0 = (0 if kind == "Q" else INNER) + i * P
                    ins = split_product(ps[:, :], lambda p, k, cc: wqkv[p][:, k, cc], slice(c0, c0 + P),
                                        lambda p, k, cc: xT[p][:, k, cc], slice(0, N))
                elif kind == "V":
                    ins = split_product(ps[:, :], lambda p, k, cc: xT[p][:, k, cc], slice(i * P, i * P + P),
                                        lambda p, k, cc: wqkv[p][:, k, cc], slice(2 * INNER, 3 * INNER))
                elif kind == "HT":
                    if i == 0:
                        pe.wait_ge(sorted_loaded, 32 * b + 32)
                    for k in range(KD):
                        for t in range(2):
                            ins = pe.transpose(ps[:, k * SEL + t * P:k * SEL + t * P + P],
                                               routed[:, i, t, k * P:k * P + P], ident[:, :])
                elif kind in ("HQ", "HK"):
                    r = 0 if kind == "HQ" else 1
                    if i == 0:
                        pe.wait_ge(hT_high, 2 * b + 1 + r)
                        wait_drained(pe, segment, b, ("HT", r))
                    w = wq_r if kind == "HQ" else wkv_r
                    for j in range(2):
                        c0 = (2 * i + j) * P
                        ins = split_product(ps[:, j * SEL:(j + 1) * SEL], lambda p, k, cc: w[p][:, k, cc],
                                            slice(c0, c0 + P), lambda p, k, cc: hT[p][:, r, k, cc], slice(0, SEL))
                elif kind == "HV":
                    ins = split_product(ps[:, :], lambda p, k, cc: hT[p][:, 1, k, cc], slice(i * P, i * P + P),
                                        lambda p, k, cc: wkv_r[p][:, k, cc], slice(INNER, 2 * INNER))
                elif kind == "LO":
                    pe.wait_ge(oT_copied, SLOTS * b + LIGHT)
                    for p in range(PAIRS):
                        ins = pe.matmul(ps[:, 0:D], loT[:, p, i * P:(i + 1) * P], wo_light[:, p, :],
                                        start=(p == 0), stop=(p == PAIRS - 1))
                elif kind == "HO":
                    pe.wait_ge(oT_copied, SLOTS * b + SLOTS)
                    for p in range(PAIRS):
                        ins = pe.matmul(ps[:, 0:D], hoT[:, p, i * P:(i + 1) * P], wo_heavy[:, p, :],
                                        start=(p == 0), stop=(p == PAIRS - 1))
                elif kind == "ZT":
                    pe.wait_ge(z_ready, b + 2)
                    for t in range(T):
                        ins = pe.transpose(ps[:, t * P:(t + 1) * P], xa[:, t, i * P:(i + 1) * P], ident[:, :])
                elif kind == "Z3":
                    pe.wait_ge(z3_ready, b)
                    for t in range(T):
                        ins = pe.transpose(ps[:, t * P:(t + 1) * P], gathered[:, t, i * P:(i + 1) * P], ident[:, :])
                elif kind == "SR":
                    pe.wait_ge(diag_ready, 2 * b + 3 + i)
                    ins = pe.matmul(ps[:, :], ones[:, :], diag.rearrange("p t n -> p (t n)"), start=True, stop=True)
                elif kind == "RK":
                    pe.wait_ge(compared, 2 * b + 3 + i)
                    for t in range(T):
                        for j in range(T):
                            pe.matmul(ps[:, t:t + 1], greater[:, j, t * P:(t + 1) * P], ones_bf[:, 0:1],
                                      start=(j == 0), stop=False)
                        ins = pe.matmul(ps[:, t:t + 1], tie[:, t, :], ones_bf[:, 0:1], start=False, stop=True)
                elif kind == "FC":
                    if i == 0:
                        pe.wait_ge(h2_high, 2 * b)
                        pe.wait_ge(h2_low, 2 * b)
                    ins = split_product(ps[:, :], lambda p, k, cc: wfcT[p][:, k, cc], slice(i * P, i * P + P),
                                        lambda p, k, cc: h2T[p][:, k, cc], slice(0, N))
                elif kind == "Y":
                    if i == 0:
                        pe.wait_ge(hid_ready, FT * b)
                    for f in range(FT):
                        ins = pe.matmul(ps[:, 0:D], hid[:, f, i * P:(i + 1) * P], wprojT[:, f, :],
                                        start=(f == 0), stop=(f == FT - 1))
                ins.then_inc(full_bank, 1)

            def scores(segment, b, s):
                if not (isinstance(b, int) and b == 0 and s < 2):
                    pe.wait_ge(exp_ready, SLOTS * b + s - 1)
                ps = ps_scores[s % 2]
                columns = score_columns(s)
                if s < LIGHT:
                    p, m = divmod(s, T)
                    if m == 0:
                        wait_drained(pe, segment, b, ("Q", p))
                        wait_drained(pe, segment, b, ("K", p))
                    for half, window in enumerate((2 * m + 1, 2 * m)):
                        lo, hi = columns[half]
                        k0 = m * P if half == 0 else (m + 1) * P - (hi - lo)
                        ins = pe.matmul(ps[:, lo:hi], qbd[:, p % 2, window, :], kT[:, p % 2, k0:k0 + hi - lo],
                                        start=True, stop=True)
                else:
                    p, j = divmod(s - LIGHT, SEL // P)
                    if j == 0 and p % 2 == 0:
                        wait_drained(pe, segment, b, ("HQ", p // 2))
                        wait_drained(pe, segment, b, ("HK", p // 2))
                    for half, (lo, hi) in enumerate(columns):
                        ins = pe.matmul(ps[:, lo:hi], qbd_r[:, p, 2 * j + half, :], kT_r[:, p, :],
                                        start=True, stop=True)
                ins.then_inc(scores_ready, 1)

            def turn(b, s):
                pe.wait_ge(probs_ready, SLOTS * b + s + 1)
                if not (isinstance(b, int) and b == 0 and s == 0):
                    pe.wait_ge(pT_copied, SLOTS * b + s)
                blocks = [(i, i) for i in range(3)] if s < LIGHT else [(0, 0), (1, 2), (2, 1), (3, 3)]
                for src, dst in blocks:
                    ins = pe.transpose(ps_pT[:, dst * P:(dst + 1) * P], probs[:, s % 2, src * P:(src + 1) * P],
                                       ident[:, :])
                ins.then_inc(pT_ready, 1)

            def attend(segment, b, s):
                pe.wait_ge(pT_copied, SLOTS * b + s + 1)
                if not (isinstance(b, int) and b == 0 and s == 0):
                    pe.wait_ge(oT_copied, SLOTS * b + s)
                if s < LIGHT:
                    p, m = divmod(s, T)
                    cols = slice(p * P, (p + 1) * P)
                    if p == 0:
                        for t in ((0, 1) if m == 0 else (m + 1,)):
                            if t < T:
                                wait_drained(pe, segment, b, ("V", t))
                    if m > 0:
                        ins = pe.matmul(ps_oT[:, 0:P], v[W:P, m - 1, cols], probsT[W:P, P:2 * P], start=True, stop=False)
                        if m < T - 1:
                            ins.then_inc(outer_done, 1)
                    pe.matmul(ps_oT[:, 0:P], v[:, m, cols], probsT[:, 2 * P:3 * P], start=(m == 0), stop=True)
                    ins = pe.matmul(ps_oT[:, P:2 * P], v[:, m, cols], probsT[:, 0:P], start=True, stop=(m == T - 1))
                    if m < T - 1:
                        if m > 0:
                            pe.wait_ge(outer_done, (T - 2) * (PAIRS * b + p) + m)
                        ins = pe.matmul(ps_oT[:, P:2 * P], v[0:W, m + 1, cols], probsT[0:W, P:2 * P],
                                        start=False, stop=True)
                else:
                    p, _ = divmod(s - LIGHT, SEL // P)
                    for t in range(2):
                        if s == LIGHT:
                            wait_drained(pe, segment, b, ("HV", t))
                        ins = pe.matmul(ps_oT[:, 0:2 * P], v_r[:, t, p * P:(p + 1) * P],
                                        probsT[:, t * 2 * P:(t + 1) * 2 * P], start=(t == 0), stop=(t == 1))
                ins.then_inc(oT_ready, 1)

            def iteration(segment, b, first=False, last=False):
                for u in slot_units(PRE, first, last):
                    unit(segment, b, u)
                scores(segment, b, 0)
                for s in range(SLOTS):
                    if s + 1 < SLOTS:
                        scores(segment, b, s + 1)
                    if s > 0:
                        attend(segment, b, s - 1)
                    for u in slot_units(s, first, last):
                        unit(segment, b, u)
                    turn(b, s)
                attend(segment, b, SLOTS - 1)
                for u in slot_units(POST, first, last):
                    unit(segment, b, u)

            pe.wait_ge(consts_made, 7)
            pe.wait_ge(silu_ready, 1)
            ps, full_bank = fill("setup", 0, ("SC", 0))
            for k in range(KD):
                ins = pe.transpose(ps[:, k * B:(k + 1) * B], silu[:, 2, k * P:(k + 1) * P], ident[0:B, 0:B])
            ins.then_inc(full_bank, 1)
            wait_drained(pe, "setup", 0, ("SC", 0))
            pe.wait_ge(wmod_loaded, 32)
            ps, full_bank = fill("setup", 0, ("MC", 0))
            for q in range(4):
                for k in range(KD):
                    ins = pe.matmul(ps[:, q * B:(q + 1) * B], raw_wmod[k][:, 3 * D + q * P:3 * D + (q + 1) * P],
                                    siluT[:, k, :], start=(k == 0), stop=(k == KD - 1))
            ins.then_inc(full_bank, 1)
            for i in range(3):
                ps, full_bank = fill("setup", 0, ("MR", i))
                for k in range(KD):
                    ins = pe.matmul(ps[0:B, :], siluT[:, k, :], raw_wmod[k][:, i * 512:(i + 1) * 512],
                                    start=(k == 0), stop=(k == KD - 1))
                ins.then_inc(full_bank, 1)
            pe.wait_ge(wmlp_loaded, 64)
            for i in range(4):
                k, g = divmod(i, 2)
                ps, full_bank = fill("setup", 0, ("WF", i))
                for t in range(4):
                    ins = pe.transpose(ps[:, t * P:(t + 1) * P], raw_wfc[g][:, t, k * P:(k + 1) * P], ident[:, :])
                ins.then_inc(full_bank, 1)
            for i in range(4):
                ps, full_bank = fill("setup", 0, ("WP", i))
                for a in range(2):
                    for dt in range(KD):
                        f = 2 * i + a
                        ins = pe.transpose(ps[:, a * D + dt * P:a * D + (dt + 1) * P],
                                           raw_wproj[dt][:, f * P:(f + 1) * P], ident[:, :])
                ins.then_inc(full_bank, 1)

            for u in SEGMENTS["start"]:
                unit("start", -1, u)
            pe.wait_ge(low_made, 10)
            pe.wait_ge(high_made, 10)
            pe.wait_ge(wo_loaded, 32)
            iteration("first", 0, first=True)
            with pe.Fori(1, B - 1) as b:
                iteration("loop", b)
            iteration("last", B - 1, last=True)
            for u in SEGMENTS["tail"]:
                unit("tail", B, u)

        @block.vector
        def _(dve):
            def drain(segment, b, unit):
                bank, before = bank_use(segment, b, unit)
                dve.wait_ge(filled[bank], before + 1)
                return ps_unit[bank], drained[bank]

            def stats1(n):
                dve.wait_ge(x_loaded, 16 * n + 16)
                for t in range(T):
                    ins = dve.bn_stats(bn6[:, 0, t, :], xa[:, t, :])
                ins.then_inc(ln_chain, 1)
                dve.wait_ge(ln_chain, 3 * n + 1)
                seal_waits(dve)
                for t in range(T):
                    ins = dve.bn_aggr(mv[:, 0, t, :], bn6[:, 0, t, :])
                ins.then_inc(mv1_ready, 1)

            def center(n):
                dve.wait_ge(mod_a_loaded, 16 * n + 16)
                dve.wait_ge(mv1_ready, n + 1)
                for t in range(T):
                    ins = dve.scalar_tensor_tensor(out=xa[:, t, :], in0=xa[:, t, :], scalar=mv[:, 0, t, 0:1],
                                                   in1=mod_a[:, 0, :], op0=ALU.subtract, op1=ALU.mult)
                ins.then_inc(ln_chain, 1)

            def modulate(n):
                dve.wait_ge(ln_chain, 3 * n + 2)
                dve.wait_ge(rstd1_ready, n + 1)
                for t in range(T):
                    ins = dve.scalar_tensor_tensor(out=h1[:, t, :], in0=xa[:, t, :], scalar=rstd[:, 0, t:t + 1],
                                                   in1=mod_a[:, 1, :], op0=ALU.mult, op1=ALU.add)
                ins.then_inc(h1_ready, 1)

            def stats2(n):
                dve.wait_ge(h1_ready, n + 1)
                for t in range(T):
                    ins = dve.bn_stats(bn6[:, 1, t, :], h1[:, t, :])
                ins.then_inc(ln_chain, 1)
                dve.wait_ge(ln_chain, 3 * n + 3)
                seal_waits(dve)
                for t in range(T):
                    ins = dve.bn_aggr(mv[:, 1, t, :], bn6[:, 1, t, :])
                ins.then_inc(mv2_ready, 1)

            def router_scores(n):
                if isinstance(n, int) and n == 0:
                    dve.wait_ge(small_loaded, 80)
                for r in range(2):
                    for t in range(T):
                        ins = dve.tensor_tensor_reduce(products[:, r, t, :], h1[:, t, :], router[:, r, :], 1.0, 0.0,
                                                       ALU.mult, ALU.add, score[:, r, t:t + 1])
                ins.then_inc(score_ready, 1)

            def second_norm(n):
                dve.wait_ge(mv2_ready, n + 1)
                dve.wait_ge(rstd2_ready, n + 1)
                for t in range(T):
                    ins = dve.tensor_scalar(xa[:, t, :], h1[:, t, :], mv[:, 1, t, 0:1], rstd[:, 1, t:t + 1],
                                            ALU.subtract, ALU.mult)
                ins.then_inc(z_ready, 1)

            def compare(segment, n, r):
                wait_drained(dve, segment, n - 1, ("SR", r))
                if r == 1:
                    wait_drained(dve, segment, n - 1, ("RK", 0))
                dve.wait_ge(score_ready, n + 1)
                for j in range(T):
                    s = score[:, r, j:j + 1]
                    e = (j + 1) * P
                    dve.tensor_scalar(greater[:, j, 0:e], score_row[:, 0:e], s, None, ALU.is_gt)
                    if j < T - 1:
                        dve.tensor_scalar(greater[:, j, e:N], score_row[:, e:N], s, None, ALU.is_ge)
                    ins = dve.scalar_tensor_tensor(out=tie[:, j, :], in0=score_row[:, j * P:e], scalar=s,
                                                   in1=later[:, :], op0=ALU.is_equal, op1=ALU.mult)
                ins.then_inc(compared, 1)

            def high_part(segment, b, unit):
                kind, k = unit
                n, highs, parts = (b + 1, xT_high, xT) if kind == "ZT" else (b - 1, h2_high, h2T)
                wait_drained(dve, segment, b, unit)
                dve.tensor_copy(parts[0][:, k, :], full[:, k, :]).then_inc(highs, 1)

            def residual(n):
                dve.wait_ge(lx_ready, T * n + T)
                dve.wait_ge(rows_gathered, 64 * n + 64)
                dve.wait_ge(final_ready, 2 * n + 1)
                dve.tensor_tensor(x2[:, :, :], lx[:, :, :], gathered[:, :, :], ALU.add).then_inc(x2_ready, 1)
                dve.wait_ge(x2_ready, n + 1)
                for t in range(T):
                    ins = dve.bn_stats(bn6[:, 2, t, :], x2[:, t, :])
                ins.then_inc(d_chain, 1)
                dve.wait_ge(d_chain, n + 1)
                seal_waits(dve)
                for t in range(T):
                    ins = dve.bn_aggr(mv[:, 2, t, :], bn6[:, 2, t, :])
                ins.then_inc(mv3_ready, 1)

            def third_norm(n):
                dve.wait_ge(mv3_ready, n + 1)
                dve.wait_ge(rstd3_ready, n + 1)
                for t in range(T):
                    ins = dve.tensor_scalar(gathered[:, t, :], x2[:, t, :], mv[:, 2, t, 0:1], rstd[:, 2, t:t + 1],
                                            ALU.subtract, ALU.mult)
                ins.then_inc(z3_ready, 1)

            def neuron(segment, b, half, step):
                n = b - 1
                base = 24 * n + 12 * half

                def after(k):
                    dve.wait_ge(lif_chain, base + k)

                yh = y[:, 2 * half:2 * half + 2, :].rearrange("p t d -> p (t d)")
                spk = spikes[:, half, :]
                if step == 1:
                    for t in (2 * half, 2 * half + 1):
                        wait_drained(dve, segment, b, ("Y", t))
                    dve.wait_ge(out_stored, 32 * n + 16)
                    if half == 1:
                        after(0)
                    dve.tensor_scalar(spk, yh, 1.0, None, ALU.is_gt).then_inc(lif_chain, 1)
                    dve.scalar_tensor_tensor(out=drive[:, :], in0=yh, scalar=-0.9, in1=yh, op0=ALU.mult,
                                             op1=ALU.subtract).then_inc(lif_chain, 1)
                    after(2)
                    dve.tensor_tensor(neg_mem[:, :], drive[:, :], spk, ALU.add).then_inc(lif_chain, 1)
                    after(3)
                    dve.scalar_tensor_tensor(out=spk, in0=neg_mem[:, :], scalar=-1.0, in1=spk, op0=ALU.is_lt,
                                             op1=ALU.add).then_inc(lif_chain, 1)
                    return
                k = 4 + 3 * (step - 2)
                dve.scalar_tensor_tensor(out=drive[:, :], in0=neg_mem[:, :], scalar=0.9, in1=yh, op0=ALU.mult,
                                         op1=ALU.subtract).then_inc(lif_chain, 1)
                after(k + 1)
                dve.scalar_tensor_tensor(out=neg_mem[:, :], in0=neg_mem[:, :], scalar=-1.0, in1=drive[:, :],
                                         op0=ALU.is_lt, op1=ALU.add).then_inc(lif_chain, 1)
                after(k + 2)
                last_step = step == STEPS - 1
                dve.scalar_tensor_tensor(out=spk, in0=neg_mem[:, :], scalar=-1.0, in1=spk, op0=ALU.is_lt,
                                         op1=ALU.add).then_inc(y_free if last_step else lif_chain, 1)

            def minimum(b, s):
                dve.wait_ge(scores_ready, SLOTS * b + s + 1)
                ps = ps_scores[s % 2]
                columns = score_columns(s)
                if columns[0][1] == columns[1][0] and columns[0][1] * 2 == columns[1][1]:
                    n = columns[1][1]
                    dve.tensor_reduce(row_min[:, s % 2, :], ps[:, 0:n].rearrange("p (a n) -> p a n", a=2), AX.X,
                                      ALU.min).then_inc(min_ready, 1)
                else:
                    for half, (lo, hi) in enumerate(columns):
                        ins = dve.tensor_reduce(row_min[:, s % 2, half:half + 1], ps[:, lo:hi], AX.X, ALU.min)
                    ins.then_inc(min_ready, 1)

            def normalize(b, s):
                dve.wait_ge(exp_ready, SLOTS * b + s + 1)
                dve.reciprocal(row_inv[:, s % 2, :], row_sum[:, s % 2, :]).then_inc(inv_ready, 1)
                dve.wait_ge(inv_ready, SLOTS * b + s + 1)
                for half, (lo, hi) in enumerate(score_columns(s)):
                    ins = dve.tensor_scalar(probs[:, s % 2, lo:hi], probs[:, s % 2, lo:hi],
                                            row_inv[:, s % 2, half:half + 1], None, ALU.mult)
                ins.then_inc(probs_ready, 1)

            def copy_out(b, s):
                dve.wait_ge(oT_ready, SLOTS * b + s + 1)
                if s < LIGHT:
                    p, m = divmod(s, T)
                    dst = loT
                else:
                    p, m = divmod(s - LIGHT, SEL // P)
                    dst = hoT
                for h in range(2):
                    rows = slice(h * DH, (h + 1) * DH)
                    ins = dve.tensor_copy(
                        dst[rows, p, m * P:(m + 1) * P].rearrange("p (w q) -> p w q", w=2),
                        ps_oT[rows, 0:2 * P].rearrange("p (w q) -> p w q", w=2)[:, :, h * W:(h + 1) * W])
                ins.then_inc(oT_copied, 1)

            def unit(segment, b, u):
                kind, i = u
                if kind == "K":
                    ps, free = drain(segment, b, u)
                    dve.tensor_copy(kT[:, i % 2, :], ps[:, :]).then_inc(free, 1)
                elif kind == "V":
                    ps, free = drain(segment, b, u)
                    dve.tensor_copy(v[:, i, :], ps[:, :]).then_inc(free, 1)
                elif kind == "HK":
                    ps, free = drain(segment, b, u)
                    dve.tensor_copy(kT_r[:, 2 * i:2 * i + 2, :], ps[:, :].rearrange("p (a n) -> p a n", a=2)
                                    ).then_inc(free, 1)
                elif kind == "HV":
                    ps, free = drain(segment, b, u)
                    dve.tensor_copy(v_r[:, i, :], ps[:, :]).then_inc(free, 1)
                elif kind == "HT":
                    ps, free = drain(segment, b, u)
                    dve.wait_ge(hT_high, 2 * b + i + 1)
                    for k in range(KD):
                        ins = dve.scalar_tensor_tensor(
                            out=hT[1][:, i, k, :], in0=ps[:, k * SEL:(k + 1) * SEL], scalar=gamma_cols[:, 1, k:k + 1],
                            in1=hT[0][:, i, k, :].bitcast(F32), op0=ALU.mult, op1=ALU.subtract)
                    ins.then_inc(free, 1)
                elif kind == "RK":
                    ps, free = drain(segment, b, u)
                    if segment != "start":
                        dve.wait_ge(rank_saved, b + 1)
                    dve.tensor_copy(rank[:, i, :], ps[:, 0:T]).then_inc(free, 1)
                elif kind == "LO":
                    ps, free = drain(segment, b, u)
                    dve.wait_ge(gate_a_loaded, 16 * b + 16)
                    if i >= 2:
                        dve.wait_ge(lx_ready, T * b + i - 1)
                    dve.tensor_tensor(lg[:, i % 2, :], ps[:, 0:D], gate_a[:, :], ALU.mult).then_inc(free, 1)
                elif kind == "HO":
                    ps, free = drain(segment, b, u)
                    dve.tensor_tensor(ho[:, i, :], ps[:, 0:D], gate_a[:, :], ALU.mult).then_inc(free, 1)
                elif kind in ("ZT", "Z3"):
                    high_part(segment, b, u)

            NEURON = {16: [(0, 1)], 17: [(0, 2)], 18: [(0, 3)], 19: [(0, 4)],
                      21: [(1, 1)], 22: [(1, 2)], 23: [(1, 3), (1, 4)]}

            def stages(segment, b, s, first, last):
                if not first:
                    if s == 3:
                        residual(b - 1)
                    if s == 4:
                        third_norm(b - 1)
                    for half, step in NEURON.get(s, []):
                        neuron(segment, b, half, step)
                if not last:
                    if s == 4:
                        stats1(b + 1)
                    if s == 5:
                        center(b + 1)
                    if s == 6:
                        modulate(b + 1)
                    if s == 7:
                        stats2(b + 1)
                    if s == 8:
                        router_scores(b + 1)
                    if s == 10:
                        second_norm(b + 1)
                    if s == 12:
                        compare(segment, b + 1, 0)
                    if s == 14:
                        compare(segment, b + 1, 1)

            def iteration(segment, b, first=False, last=False):
                for u in slot_units(PRE, first, last):
                    unit(segment, b, u)
                minimum(b, 0)
                for s in range(SLOTS):
                    if s + 1 < SLOTS:
                        minimum(b, s + 1)
                    normalize(b, s)
                    if s > 0:
                        copy_out(b, s - 1)
                    for u in slot_units(s, first, last):
                        unit(segment, b, u)
                    stages(segment, b, s, first, last)
                copy_out(b, SLOTS - 1)
                for u in slot_units(POST, first, last):
                    unit(segment, b, u)

            step = [0]

            def link(ins):
                step[0] += 1
                ins.then_inc(setup_chain, 1)
                dve.wait_ge(setup_chain, step[0])

            dve.wait_ge(exp_c, 1)
            link(dve.tensor_scalar(silu[:, 1, :], silu[:, 1, :], 1.0, None, ALU.add))
            link(dve.reciprocal(silu[:, 1, :], silu[:, 1, :]))
            dve.tensor_tensor(silu[:, 2, :], silu[:, 0, :], silu[:, 1, :], ALU.mult).then_inc(silu_ready, 1)
            dve.memset(probs[:, :, :], 0.0).then_inc(zeros_made, 1)
            dve.memset(qbd[:, :, :, :], 0.0).then_inc(zeros_made, 1)
            dve.memset(marks[:, 1:2], 0.0).then_inc(y_free, 2)
            dve.memset(marks[:, 2:3], 0.0).then_inc(out_stored, 16)
            ps, free = drain("setup", 0, ("SC", 0))
            dve.tensor_copy(siluT[:, :, :], ps[:, 0:KD * B].rearrange("p (k b) -> p k b", k=KD)).then_inc(free, 1)
            stats1(0)
            ps, free = drain("setup", 0, ("MC", 0))
            cols = ps[:, 0:4 * B].rearrange("p (q b) -> p q b", q=4)
            dve.tensor_copy(shift_b[:, :, :], cols[:, 0:KD, :])
            dve.tensor_scalar(scale_b[:, :, :], cols[:, KD:2 * KD, :], 1.0, None, ALU.add).then_inc(free, 1)
            ps, free = drain("setup", 0, ("MR", 0))
            dve.tensor_copy(mod_norm[:, D:2 * D], ps[0:B, 0:D])
            dve.tensor_scalar(mod_norm[:, 0:D], ps[0:B, D:2 * D], 1.0, None, ALU.add).then_inc(free, 1)
            ps, free = drain("setup", 0, ("MR", 1))
            dve.tensor_copy(gates[:, 0:D], ps[0:B, 0:D]).then_inc(free, 1)
            ps, free = drain("setup", 0, ("MR", 2))
            dve.tensor_copy(gates[:, D:2 * D], ps[0:B, D:2 * D]).then_inc(free, 1)
            wait_drained(dve, "setup", 0, ("MR", 1))
            wait_drained(dve, "setup", 0, ("MR", 2))
            link(dve.scalar_tensor_tensor(out=gates_abs, in0=gates, scalar=-1.0, in1=gates, op0=ALU.mult, op1=ALU.max))
            link(dve.tensor_scalar(gates_abs, gates_abs, 0.25, None, ALU.max))
            link(dve.tensor_scalar(gates_sign, gates, 0.0, 2.0, ALU.is_ge, ALU.mult))
            link(dve.scalar_tensor_tensor(out=mod_gate, in0=gates_sign, scalar=-1.0, in1=gates_abs,
                                          op0=ALU.add, op1=ALU.mult))
            dve.tensor_scalar(mod_gate[:, D:2 * D], mod_gate[:, D:2 * D], 1.0 / STEPS, None,
                              ALU.mult).then_inc(mod_ready, 1)
            center(0)
            modulate(0)
            stats2(0)
            router_scores(0)
            for k in range(KD):
                dve.wait_ge(high_made, k + 1)
                dve.tensor_tensor(wqkv[1][:, k, :], raw_wqkv[:, k, :], wqkv[0][:, k, :].bitcast(F32),
                                  ALU.subtract).then_inc(low_made, 1)
            second_norm(0)
            for k in range(KD):
                dve.wait_ge(high_made, 3 + 2 * k)
                dve.tensor_tensor(wq_r[1][:, k, :], raw_wq[:, k, :], wq_r[0][:, k, :].bitcast(F32),
                                  ALU.subtract).then_inc(low_made, 1)
                dve.wait_ge(high_made, 4 + 2 * k)
                dve.tensor_tensor(wkv_r[1][:, k, :], raw_wkv[k], wkv_r[0][:, k, :].bitcast(F32),
                                  ALU.subtract).then_inc(low_made, 1)
            dve.tensor_scalar(gamma_cols[:, 1, :], gamma_cols[:, 0, :], float(D) ** 0.5, None,
                              ALU.mult).then_inc(low_made, 1)
            for i in range(4):
                ps, free = drain("setup", 0, ("WF", i))
                dve.wait_ge(high_made, 7 + i)
                cols = slice((i % 2) * 512, (i % 2 + 1) * 512)
                dve.tensor_tensor(wfcT[1][:, i // 2, cols], ps[:, :], wfcT[0][:, i // 2, cols].bitcast(F32),
                                  ALU.subtract).then_inc(free, 1)
            for i in range(4):
                wait_drained(dve, "setup", 0, ("WF", i))
            dve.memset(marks[:, 0:1], 0.0).then_inc(low_made, 3)
            high_part("start", -1, ("ZT", 0))
            high_part("start", -1, ("ZT", 1))
            for r in range(2):
                compare("start", 0, r)
                unit("start", -1, ("RK", r))
            dve.wait_ge(mod_stored, 32)
            iteration("first", 0, first=True)
            with dve.Fori(1, B - 1) as b:
                iteration("loop", b)
            iteration("last", B - 1, last=True)
            residual(B - 1)
            third_norm(B - 1)
            for k in range(KD):
                high_part("tail", B, ("Z3", k))
            for half in range(2):
                for s in range(1, STEPS):
                    neuron("tail", B, half, s)


_INS = ["L0_attn_x", "L0_attn_gamma_h", "L0_attn_wq_h", "L0_attn_wkv_h", "L0_attn_wo_h", "L0_attn_ln_g",
        "L0_attn_ln_b", "L0_attn_wqkv_l", "L0_attn_wo_l", "L0_attn_rt_q", "L0_attn_rt_kv", "L0_ffn_W_fc",
        "L0_ffn_W_proj", "L0_c", "L0_wmod"]


def kernel(**inputs):
    import numpy as _np
    import concourse.bacc as _bacc
    from concourse import mybir as _mybir
    from concourse.bass_utils import run_bass_kernel_spmd as _run

    nc = _bacc.Bacc("TRN2", target_bir_lowering=False, num_devices=1)
    arrays, args = {}, []
    for name in _INS:
        a = _np.ascontiguousarray(inputs[name])
        arrays[f"in_{name}"] = a
        args.append(nc.dram_tensor(f"in_{name}", a.shape, _mybir.dt.from_np(a.dtype), kind="ExternalInput").ap())
    args.append(nc.dram_tensor("out_x", (B, N, D), F32, kind="ExternalOutput").ap())
    adaln_block_kernel(nc, *args)
    return _run(nc, [arrays], core_ids=[0]).results[0]["out_x"]
```

```python
from contextlib import ExitStack

import concourse.bass as bass
from concourse import mybir

F32 = mybir.dt.float32
F32R = mybir.dt.float32r
BF16 = mybir.dt.bfloat16
I32 = mybir.dt.int32
ALU = mybir.AluOpType
ACT = mybir.ActivationFunctionType
AX = mybir.AxisListType

P = 128
B, N, D = 8, 512, 256
H, DH = 8, 64
INNER = H * DH
W = 64
SEL = 256
F = 4 * D
STEPS = 5
T = N // P
KD = D // P
PAIRS = H // 2
NW = N // W
FT = F // P
WF_HIGH = 3 * KD
LOW_PARTS = 3 * KD + 1
LIGHT = PAIRS * T
HEAVY = PAIRS * (SEL // P)
SLOTS = LIGHT + HEAVY
SCALE = DH ** -0.5
BANKS = 2

SLOT_UNITS = {
    0: [("HT", 0)],
    1: [("V", 3), ("HO", 0), ("HO", 1)],
    2: [("HT", 1)],
    3: [("Q", 2), ("HV", 1)],
    4: [("K", 2)],
    5: [],
    6: [("Q", 3), ("K", 3)],
    7: [("Z3", 0), ("Z3", 1)],
    8: [("HV", 0), ("FC", 0), ("FC", 1)],
    9: [("HQ", 0), ("FC", 2), ("YA", 0)],
    10: [("FC", 3), ("YA", 1), ("SR", 0)],
    11: [("FC", 4), ("YA", 2)],
    12: [("FC", 5), ("YA", 3), ("HK", 0)],
    13: [("RK", 0), ("FC", 6), ("YA", 4), ("SR", 1)],
    14: [("FC", 7), ("YA", 5)],
    15: [("YA", 6), ("ZT", 0)],
    16: [("YA", 7), ("ZT", 1), ("RK", 1)],
    17: [("HQ", 1), ("HK", 1)],
    18: [("LO", 0), ("NQ", 0)],
    19: [("LO", 1), ("NK", 0)],
    20: [("LO", 2), ("NV", 0)],
    21: [("LO", 3), ("NQ", 1)],
    22: [("NV", 1), ("NV", 2), ("NK", 1)],
    23: [],
}
FIRST_UNITS = {8: [("WF", 0), ("WF", 1)], 9: [("WF", 2)], 10: [("WF", 3), ("WP", 0)], 11: [("WP", 1)],
               12: [("WP", 2)], 13: [("WP", 3)]}
FIRST_WEIGHTS = [u for units in FIRST_UNITS.values() for u in units]
MLP_UNITS = ("HO", "Z3", "FC", "YA")
NEXT_UNITS = ("ZT", "SR", "RK", "NQ", "NK", "NV")


PROJECTED_AHEAD = [("NQ", 1), ("NK", 1), ("NV", 0), ("NV", 1), ("NV", 2)]


def slot_units(slot, first, last):
    units = [u for u in SLOT_UNITS[slot]
             if not (first and u[0] in MLP_UNITS) and not (last and u[0] in NEXT_UNITS)]
    return units + FIRST_UNITS.get(slot, []) if first else units


def iteration_units(first, last):
    return [u for s in range(SLOTS) for u in slot_units(s, first, last)]


SEGMENTS = {
    "setup": [("SC", 0), ("MB", 0), ("MC", 0)] + [("MR", i) for i in range(3)],
    "start": [("ZT", 0), ("ZT", 1), ("SR", 0), ("NQ", 0), ("NK", 0), ("RK", 0), ("NV", 0), ("SR", 1), ("NV", 1),
              ("NQ", 1), ("NV", 2), ("RK", 1), ("NK", 1)],
    "first": iteration_units(True, False),
    "loop": iteration_units(False, False),
    "last": iteration_units(False, True),
    "tail": [("HO", 0), ("HO", 1), ("Z3", 0), ("Z3", 1), ("FC", 0), ("FC", 1), ("FC", 2), ("YA", 0),
             ("Z3", 2), ("Z3", 3)]
            + [u for i in range(3, 2 * FT) for u in (("FC", i), ("YA", i - 2))]
            + [("YA", 2 * FT - 2), ("YA", 2 * FT - 1)],
}
BANKED = {s: [u for u in units if u[0] != "YA"] for s, units in SEGMENTS.items()}
USES = {s: [len(u[k::BANKS]) for k in range(BANKS)] for s, u in BANKED.items()}


def bank_use(segment, b, unit):
    i = BANKED[segment].index(unit)
    bank, before = i % BANKS, i // BANKS
    for s in BANKED:
        if s == segment:
            break
        before += USES[s][bank] * (B - 2 if s == "loop" else 1)
    if segment == "loop":
        return bank, b * USES["loop"][bank] + (before - USES["loop"][bank])
    return bank, before


def chunk_tokens(segment, i):
    if segment == "tail":
        half, f = divmod(i, FT)
        return f, slice(half * N // 2, (half + 1) * N // 2)
    return i, slice(0, N)


def norm_tokens(segment, i):
    half, k = divmod(i, KD)
    tiles = half_tiles(half if segment == "tail" else None)
    return k, tiles, slice(tiles.start * P, tiles.stop * P)


def half_tiles(half):
    return range(T) if half is None else range(half * T // 2, (half + 1) * T // 2)


def score_columns(s):
    if s >= LIGHT:
        return (0, SEL), (SEL, 2 * SEL)
    m = s % T
    return (0, P if m == T - 1 else P + W), (2 * P if m == 0 else P + W, 3 * P)


def adaln_block_kernel(nc, x, gamma_h, wq_h, wkv_h, wo_h, ln_g, ln_b, wqkv_l, wo_l, rt_q, rt_kv,
                       w_fc, w_proj, c, wmod, out):
    with ExitStack() as ctx:
        def sb(name, shape, dt=F32):
            return ctx.enter_context(nc.sbuf_tensor(name, shape, dt))

        def sem(name):
            return ctx.enter_context(nc.semaphore(name))

        mod_rows = nc.dram_tensor("mod_rows", [B, 4 * D], F32, kind="Internal").ap()
        sorted_rows = [nc.dram_tensor(f"sorted_rows{r}", [N, D], F32, kind="Internal").ap() for r in range(2)]
        routed_out = nc.dram_tensor("routed_out", [N, D], F32, kind="Internal").ap()

        ident = sb("ident", [P, P])
        ones_bf = sb("ones_bf", [P, 2], BF16)
        later = sb("later", [P, P], BF16)
        neg_half = sb("neg_half", [P, T])
        router = sb("router", [P, 2, D])
        ln_cols = sb("ln_cols", [P, 2, KD])
        gamma_cols = sb("gamma_cols", [P, 2, KD])
        shift_b = sb("shift_b", [P, KD, B])
        scale_b = sb("scale_b", [P, KD, B])
        wqkv = [sb(f"wqkv{i}", [P, KD, 3 * INNER], F32R) for i in range(2)]
        wq_r = [sb(f"wq_r{i}", [P, KD, INNER], F32R) for i in range(2)]
        wkv_r = [sb(f"wkv_r{i}", [P, KD, 2 * INNER], F32R) for i in range(2)]
        wfcT = [sb(f"wfcT{i}", [P, KD, F], F32R) for i in range(2)]
        wprojT = [sb(f"wprojT{i}", [P, FT, D], F32R) for i in range(2)]
        wo_light = sb("wo_light", [P, PAIRS, D])
        wo_heavy = sb("wo_heavy", [P, PAIRS, D])

        xa = sb("xa", [P, T, D])
        h1 = sb("h1", [P, T, D])
        hn = sb("hn", [P, T, D])
        bn6 = sb("bn6", [P, 3, T, 6])
        mv = sb("mv", [P, 3, T, 2])
        veps = sb("veps", [P, 4, T])
        rstd = sb("rstd", [P, 4, T])
        musq = sb("musq", [P, T])
        score = sb("score", [P, 2, T])
        marks = sb("marks", [P, 4])
        full = sb("full", [P, 2, N])
        xT = [sb(f"xT{i}", [P, KD, N], F32R) for i in range(2)]
        rank = sb("rank", [P, 2, T], I32)
        rank_kept = sb("rank_kept", [P, T], I32)
        mod_a = full[:, 0, :].rearrange("p (a d) -> p a d", a=2)
        late = sb("late", [P, 1792])
        score_row = late[:, 0:512]
        greater = late[:, 512:1536].bitcast(BF16).rearrange("p (t n) -> p t n", t=T)
        tie = late[:, 1536:1792].bitcast(BF16).rearrange("p (t n) -> p t n", t=T)

        qbd = sb("qbd", [P, 2, NW, P])
        kT = sb("kT", [P, 2, N])
        v = sb("v", [P, T, INNER])
        v_r = sb("v_r", [P, SEL // P, INNER])
        probs = sb("probs", [P, 3, 512])
        probsT = sb("probsT", [P, 512])
        row_min = sb("row_min", [P, 3, 2])
        row_sum = sb("row_sum", [P, 3, 2])
        row_inv = sb("row_inv", [P, 3, 2])
        loT = sb("loT", [P, PAIRS, N])
        routed = sb("routed", [P, 2, 2, D])
        products = routed[:, 0, :, :].rearrange("p t d -> p (t d)").bitcast(BF16).rearrange(
            "p (t n) -> p t n", t=T)

        qbd_r = qbd[:, :, :, :].rearrange("p a (c w) q -> p (a c) w q", c=2)
        kT_r = kT[:, :, :].rearrange("p a (c n) -> p (a c) n", c=2)
        hoT = late[:, 0:1024].rearrange("p (t n) -> p t n", t=PAIRS)
        ho = late[:, 1024:1536].rearrange("p (t n) -> p t n", t=2)

        gate_a = sb("gate_a", [P, D])
        gate_b = sb("gate_b", [P, D])
        lx = sb("lx", [P, T, D])
        gathered = hn
        x2 = sb("x2", [P, T, D])
        h2T = xT
        hT = [sb(f"hT{i}", [P, 2, KD, SEL], F32R) for i in range(2)]
        hid = sb("hid", [P, 3, N])
        hid_parts = [sb(f"hid_parts{i}", [P, 2, N], F32R) for i in range(2)]
        hid_relu = hid[:, 0:2, :]
        lg = hid[:, 0, :].rearrange("p (a d) -> p a d", a=2)
        hid_square = hid[:, 2, :]
        spikes = sb("spikes", [P, 2, 2 * D])
        membrane = sb("membrane", [P, 2, 2 * D])
        drive, neg_mem = membrane[:, 0, :], membrane[:, 1, :]

        raw_wmod = [loT[:, 0:3, :].rearrange("p t n -> p (t n)"), late[:, 0:1536]]
        raw_wqkv = [hid[:, :, :].rearrange("p t n -> p (t n)"),
                    qbd[:, :, :, :].rearrange("p a w q -> p (a w q)")[:, 0:1536]]
        raw_wq = loT[:, 2:4, :]
        raw_wkv = [hid[:, 0:2, :].rearrange("p t n -> p (t n)"), v_r[:, :, :].rearrange("p t n -> p (t n)")]
        raw_wfc = [x2[:, :, :], spikes[:, :, :].rearrange("p a n -> p (a n)").rearrange("p (t d) -> p t d", t=T)]
        raw_wproj = [membrane[:, :, :].rearrange("p a n -> p (a n)"), lx[:, :, :].rearrange("p a n -> p (a n)")]
        silu = hn[0:B, 0:3, :]
        siluT = sb("siluT", [P, KD, B])
        silu_first = h1[:, 0, :].rearrange("p (k n) -> p k n", k=KD)
        mod_norm, mod_gate, gates, gates_abs = (v[0:B, i, :] for i in range(4))
        gates_sign = probsT[0:B, :]

        ps_scores = [ctx.enter_context(nc.psum_tensor(f"ps_scores{i}", [P, 512], F32)) for i in range(2)]
        ps_pT = ctx.enter_context(nc.psum_tensor("ps_pT", [P, 512], F32))
        ps_oT = ctx.enter_context(nc.psum_tensor("ps_oT", [P, 512], F32))
        ps_y = [ctx.enter_context(nc.psum_tensor(f"ps_y{i}", [P, 512], F32)) for i in range(2)]
        ps_unit = [ctx.enter_context(nc.psum_tensor(f"ps_unit{i}", [P, 512], F32)) for i in range(BANKS)]

        filled = [sem(f"filled{i}") for i in range(BANKS)]
        drained = [sem(f"drained{i}") for i in range(BANKS)]
        consts_made = sem("consts_made")
        zeros_made = sem("zeros_made")
        zero_rows_stored = sem("zero_rows_stored")
        x_loaded = sem("x_loaded")
        mod_a_loaded = sem("mod_a_loaded")
        small_loaded = sem("small_loaded")
        c_loaded = sem("c_loaded")
        wmod_norm_loaded = sem("wmod_norm_loaded")
        wmod_rest_loaded = sem("wmod_rest_loaded")
        wqkv_loaded = sem("wqkv_loaded")
        wr_loaded = sem("wr_loaded")
        wmlp_loaded = sem("wmlp_loaded")
        wo_loaded = sem("wo_loaded")
        exp_c = sem("exp_c")
        setup_chain = sem("setup_chain")
        silu_ready = sem("silu_ready")
        mod_stored = sem("mod_stored")
        mod_ready = sem("mod_ready")
        high_made = sem("high_made")
        low_made = sem("low_made")
        scores_ready = sem("scores_ready")
        min_ready = sem("min_ready")
        exp_ready = sem("exp_ready")
        inv_ready = sem("inv_ready")
        probs_ready = sem("probs_ready")
        pT_ready = sem("pT_ready")
        pT_copied = sem("pT_copied")
        outer_done = sem("outer_done")
        oT_ready = sem("oT_ready")
        oT_copied = sem("oT_copied")
        ln_chain = sem("ln_chain")
        mv1_ready = sem("mv1_ready")
        mv2_ready = sem("mv2_ready")
        mv3_ready = sem("mv3_ready")
        pool_chain = sem("pool_chain")
        norm_ready = sem("norm_ready")
        pool_chain3 = sem("pool_chain3")
        rstd1_ready = sem("rstd1_ready")
        rstd2_ready = sem("rstd2_ready")
        rstd3_ready = sem("rstd3_ready")
        h1_ready = sem("h1_ready")
        hn_ready = sem("hn_ready")
        score_ready = sem("score_ready")
        z_ready = sem("z_ready")
        xT_high = sem("xT_high")
        xT_low = sem("xT_low")
        diag_ready = sem("diag_ready")
        compared = sem("compared")
        scattered = sem("scattered")
        sorted_loaded = sem("sorted_loaded")
        rank_saved = sem("rank_saved")
        hT_high = sem("hT_high")
        lx_loaded = sem("lx_loaded")
        gate_a_loaded = sem("gate_a_loaded")
        gate_b_loaded = sem("gate_b_loaded")
        lx_ready = sem("lx_ready")
        ho_stored = sem("ho_stored")
        rows_gathered = sem("rows_gathered")
        tail_gathered = sem("tail_gathered")
        x2_ready = sem("x2_ready")
        d_chain = sem("d_chain")
        z3_ready = sem("z3_ready")
        h2_high = sem("h2_high")
        h2_low = sem("h2_low")
        hid_squared = sem("hid_squared")
        hid_high = sem("hid_high")
        hid_low = sem("hid_low")
        tail_squared = sem("tail_squared")
        tail_low = sem("tail_low")
        hid_used = sem("hid_used")
        y_negated = sem("y_negated")
        lif_chain = sem("lif_chain")
        y_free = sem("y_free")
        out_chain = sem("out_chain")
        final_ready = sem("final_ready")
        waits_passed = sem("waits_passed")
        out_stored = sem("out_stored")

        def wait_drained(eng, segment, b, *units):
            last = {}
            for u in sorted(units, key=BANKED[segment].index):
                bank, before = bank_use(segment, b, u)
                last[bank] = before + 1
            for bank, count in last.items():
                eng.wait_ge(drained[bank], count)

        def mlp_weight(part, unit):
            kind, i = unit
            if kind == "WF":
                return wfcT[part][:, i // 2, (i % 2) * 512:(i % 2 + 1) * 512]
            return wprojT[part][:, 2 * i:2 * i + 2, :].rearrange("p a n -> p (a n)")

        def low_made_of(segment, b, i):
            if segment != "tail":
                return hid_low, FT * (b - 1) + i + 1
            return (tail_low, i // 2 + 1) if i % 2 else (hid_low, FT * (B - 1) + i // 2 + 1)

        def square_low(eng, segment, b, i):
            _, cols = chunk_tokens(segment, i)
            low, count = low_made_of(segment, b, i)
            squared, square = (hid_squared, hid_square[:, cols]) if low is hid_low else \
                (tail_squared, hid_square[:, N // 2:N])
            if segment == "tail" and i % 2 == 0:
                square = hid_square[:, 0:N // 2]
            wait_drained(eng, segment, b, ("FC", i))
            if segment == "tail" and i == 1:
                eng.wait_ge(hid_low, FT * (B - 1))
            elif segment == "tail" or i > 0:
                eng.wait_ge(low, count - 1)
            eng.tensor_tensor(square, hid_relu[:, i % 2, cols], hid_relu[:, i % 2, cols],
                              ALU.mult).then_inc(squared, 1)
            eng.wait_ge(squared, count)
            eng.wait_ge(hid_high, FT * (b - 1) + i + 1)
            eng.tensor_tensor(hid_parts[1][:, i % 2, cols], square, hid_parts[0][:, i % 2, cols].bitcast(F32),
                              ALU.subtract).then_inc(low, 1)

        def final(eng, n, half):
            sp2 = spikes[:, half, :].rearrange("p (t d) -> p t d", t=2)
            eng.wait_ge(gate_b_loaded, 16 * n + 16)
            eng.wait_ge(y_free, 2 * n + half + 3)
            eng.tensor_tensor(sp2, sp2, gate_b[:, :].unsqueeze(1).to_broadcast([P, 2, D]),
                              ALU.mult).then_inc(out_chain, 1)
            eng.wait_ge(out_chain, 2 * n + half + 1)
            eng.tensor_tensor(sp2, sp2, x2[:, 2 * half:2 * half + 2, :], ALU.add).then_inc(final_ready, 1)

        def seal_waits(eng):
            eng.sem_inc(waits_passed, 1)

        block = ctx.enter_context(nc.Block())

        @block.sync
        def _(sp):
            sp.dma_start(silu[:, 0, :], c).then_inc(c_loaded, 16)
            def load_wmod(columns, loaded):
                for k in range(KD):
                    sp.dma_start(raw_wmod[k][:, columns], wmod[k * P:(k + 1) * P, columns]).then_inc(loaded, 16)

            load_wmod(slice(0, 2 * D), wmod_norm_loaded)
            sp.dma_start(xa[:, :, :], x[0].rearrange("(t p) d -> p t d", p=P)).then_inc(x_loaded, 16)
            for k in range(KD):
                sp.dma_start(raw_wqkv[k], wqkv_l[k * P:(k + 1) * P, :]).then_inc(wqkv_loaded, 16)
            for i, a in enumerate((rt_q, rt_kv)):
                sp.dma_start(router[:, i, :], a.partition_broadcast(P)).then_inc(small_loaded, 16)
            load_wmod(slice(2 * D, 6 * D), wmod_rest_loaded)
            sp.dma_start(raw_wkv[1], wkv_h[P:2 * P, :]).then_inc(wr_loaded, 16)
            sp.wait_ge(zeros_made, 1)
            sp.dma_start(routed_out[0:SEL, :].rearrange("(p r) d -> p (r d)", p=P),
                         probs[:, 0, :]).then_inc(zero_rows_stored, 16)
            sp.dma_start(wo_light[:, :, :], wo_l.rearrange("(t p) n -> p t n", p=P)).then_inc(wo_loaded, 16)
            sp.dma_start(wo_heavy[:, :, :], wo_h.rearrange("(t p) n -> p t n", p=P)).then_inc(wo_loaded, 16)
            for i in range(2):
                sp.dma_start(raw_wfc[i],
                             w_fc[i * 512:(i + 1) * 512, :].rearrange("(t p) d -> p t d", p=P)
                             ).then_inc(wmlp_loaded, 16)
                sp.dma_start(raw_wproj[i], w_proj[i * P:(i + 1) * P, :]).then_inc(wmlp_loaded, 16)
            wait_drained(sp, "setup", 0, ("MR", 2))
            sp.dma_start(raw_wq, wq_h.rearrange("(k p) n -> p k n", p=P)).then_inc(wr_loaded, 16)
            sp.wait_ge(low_made, KD)
            sp.dma_start(raw_wkv[0], wkv_h[0:P, :]).then_inc(wr_loaded, 16)
            sp.wait_ge(mod_ready, 1)
            sp.dma_start(mod_rows[:, 0:2 * D], mod_norm).then_inc(mod_stored, 16)
            sp.dma_start(mod_rows[:, 2 * D:4 * D], mod_gate).then_inc(mod_stored, 16)
            sp.wait_ge(mod_stored, 32)

            def mod_row(n, first, last):
                row = mod_rows[n:n + 1, first * D:last * D] if isinstance(n, int) else \
                    mod_rows[bass.ds(n, 1), first * D:last * D]
                return row.rearrange("a n -> (a n)").partition_broadcast(P)

            def batch(t, n):
                a = t[n:n + 1] if isinstance(n, int) else t[bass.ds(n, 1)]
                return a.rearrange("a (t p) d -> p (a t) d", p=P)

            def load_sorted(segment, n):
                sp.wait_ge(scattered, 128 * n + 128)
                seal_waits(sp)
                if segment != "start":
                    wait_drained(sp, segment, n - 1, ("HT", 1))
                for r in range(2):
                    sp.dma_start(routed[:, r, :, :], sorted_rows[r][N - SEL:N, :].rearrange(
                        "(t p) d -> p t d", p=P)).then_inc(sorted_loaded, 16)

            def store(n, half):
                sp.wait_ge(final_ready, 2 * n + half + 2)
                sp.dma_start(batch(out, n)[:, 2 * half:2 * half + 2, :],
                             spikes[:, half, :].rearrange("p (t d) -> p t d", t=2)).then_inc(out_stored, 16)

            def store_ho(segment, b):
                for t in range(2):
                    wait_drained(sp, segment, b, ("HO", t))
                    seal_waits(sp)
                sp.dma_start(routed_out[N - SEL:N, :].rearrange("(t p) d -> p t d", p=P),
                             ho).then_inc(ho_stored, 16)

            def iteration(segment, b, first=False, last=False):
                if not last:
                    sp.wait_ge(xT_high, 2 * b + 2)
                    sp.dma_start(xa[:, :, :], batch(x, b + 1)).then_inc(x_loaded, 16)
                    sp.wait_ge(xT_low, 2 * b + 2)
                    sp.dma_start(mod_a[:, :, :].rearrange("p a d -> p (a d)"),
                                 mod_row(b + 1, 0, 2)).then_inc(mod_a_loaded, 16)
                if not first:
                    sp.wait_ge(final_ready, 2 * b - 1)
                    sp.dma_start(gate_b[:, :], mod_row(b - 1, 3, 4)).then_inc(gate_b_loaded, 16)
                    store_ho(segment, b)
                sp.dma_start(gate_a[:, :], mod_row(b, 2, 3)).then_inc(gate_a_loaded, 16)
                if not first:
                    sp.wait_ge(x2_ready, b)
                else:
                    wait_drained(sp, segment, b, ("WP", 3))
                sp.dma_start(lx[:, :, :], batch(x, b)).then_inc(lx_loaded, 16)
                if not last:
                    load_sorted(segment, b + 1)
                if not first:
                    store(b - 1, 0)
                    store(b - 1, 1)

            load_sorted("start", 0)
            iteration("first", 0, first=True)
            with sp.Fori(1, B - 1) as b:
                iteration("loop", b)
            iteration("last", B - 1, last=True)
            sp.wait_ge(final_ready, 2 * B - 1)
            sp.dma_start(gate_b[:, :], mod_row(B - 1, 3, 4)).then_inc(gate_b_loaded, 16)
            store_ho("tail", B)
            store(B - 1, 0)
            store(B - 1, 1)
            sp.wait_ge(out_stored, 32 * B + 16)

        @block.gpsimd
        def _(pool):
            pool.memset(ident[:, :], 0.0).then_inc(consts_made, 1)
            pool.memset(later[:, :], 1.0).then_inc(consts_made, 1)
            pool.memset(ones_bf[:, :], 1.0).then_inc(consts_made, 1)
            pool.memset(neg_half[:, :], -0.5).then_inc(consts_made, 1)
            pool.wait_ge(consts_made, 2)
            pool.affine_select(out=ident[:, :], in_=ident[:, :], compare_op=ALU.not_equal, fill=1.0, base=0,
                               pattern=[[-1, P]], channel_multiplier=1).then_inc(consts_made, 1)
            pool.affine_select(out=later[:, :], in_=later[:, :], compare_op=ALU.is_gt, fill=0.0, base=0,
                               pattern=[[1, P]], channel_multiplier=-1).then_inc(consts_made, 1)
            pool.memset(veps[:, :, :], 1.0).then_inc(final_ready, 1)
            pool.memset(probs[:, :, :], 0.0).then_inc(zeros_made, 1)
            pool.wait_ge(consts_made, 6)
            pool.wait_ge(final_ready, 1)

            def rstd_of(i, chain, count, tiles=range(T)):
                ts = slice(tiles.start, tiles.stop)
                pool.tensor_scalar(veps[:, i, ts], mv[:, i, ts, 1], 1e-5, 1.0, ALU.add, ALU.mult).then_inc(chain, 1)
                pool.wait_ge(chain, count)
                return pool.tensor_tensor(rstd[:, i, ts], veps[:, i, ts], neg_half[:, ts], ALU.pow)

            def rstd1(n):
                pool.wait_ge(mv1_ready, n + 1)
                seal_waits(pool)
                rstd_of(0, pool_chain, 5 * n + 1).then_inc(rstd1_ready, 1)

            def rstd2(n):
                pool.wait_ge(mv2_ready, n + 1)
                seal_waits(pool)
                rstd_of(1, pool_chain, 5 * n + 2).then_inc(rstd2_ready, 1)
                pool.tensor_tensor(musq[:, :], mv[:, 1, :, 0], mv[:, 1, :, 0], ALU.mult).then_inc(pool_chain, 1)
                pool.wait_ge(pool_chain, 5 * n + 3)
                pool.tensor_tensor(musq[:, :], musq[:, :], mv[:, 1, :, 1], ALU.add).then_inc(pool_chain, 1)
                pool.wait_ge(pool_chain, 5 * n + 4)
                seal_waits(pool)
                pool.tensor_scalar(veps[:, 3, :], musq[:, :], float(D), 1e-24, ALU.mult, ALU.max).then_inc(pool_chain, 1)
                pool.wait_ge(pool_chain, 5 * n + 5)
                pool.tensor_tensor(rstd[:, 3, :], veps[:, 3, :], neg_half[:, :], ALU.pow).then_inc(norm_ready, 1)

            def norm_rows(segment, n):
                pool.wait_ge(h1_ready, n + 1)
                if segment == "loop":
                    wait_drained(pool, segment, n - 1, ("Z3", 1))
                pool.wait_ge(norm_ready, n + 1)
                seal_waits(pool)
                for t in range(T):
                    ins = pool.tensor_scalar(hn[:, t, :], h1[:, t, :], rstd[:, 3, t:t + 1], 1.0, ALU.mult, ALU.mult)
                ins.then_inc(hn_ready, 1)

            def scatter(segment, n, r, t):
                if t == 0:
                    wait_drained(pool, segment, n - 1, ("RK", r))
                    pool.wait_ge(hn_ready, n + 1)
                    if not (isinstance(n, int) and n == 0):
                        pool.wait_ge(sorted_loaded, 32 * n)
                    seal_waits(pool)
                pool.indirect_dma_start(out=sorted_rows[r], out_offset=bass.IndirectOffsetOnAxis(
                    ap=rank[:, r, t:t + 1], axis=0), in_=hn[:, t, :], in_offset=None).then_inc(scattered, 16)

            def save_rank(n):
                if not (isinstance(n, int) and n == 0):
                    pool.wait_ge(rows_gathered, 64 * n)
                pool.wait_ge(scattered, 128 * n + 128)
                seal_waits(pool)
                pool.tensor_copy(rank_kept[:, :], rank[:, 0, :]).then_inc(rank_saved, 1)

            def gather(n, last, in_tail=False):
                pool.wait_ge(rank_saved, n + 1)
                pool.wait_ge(ho_stored, 16 * n + 16)
                if not last:
                    pool.wait_ge(scattered, 128 * n + 256)
                seal_waits(pool)
                for t in range(T):
                    there = tail_gathered if in_tail and t >= T // 2 else rows_gathered
                    pool.indirect_dma_start(out=gathered[:, t, :], out_offset=None, in_=routed_out,
                                            in_offset=bass.IndirectOffsetOnAxis(ap=rank_kept[:, t:t + 1], axis=0)
                                            ).then_inc(there, 16)

            def rstd3(n, half=None):
                count = n + 1 + (half or 0)
                pool.wait_ge(mv3_ready, count)
                seal_waits(pool)
                rstd_of(2, pool_chain3, count, half_tiles(half)).then_inc(rstd3_ready, 1)

            def low_part(segment, b, k):
                wait_drained(pool, segment, b, ("ZT", k))
                pool.wait_ge(xT_high, 2 * b + k + 3)
                pool.tensor_tensor(xT[1][:, k, :], full[:, k, :], xT[0][:, k, :].bitcast(F32),
                                   ALU.subtract).then_inc(xT_low, 1)

            def add_x(segment, b, t):
                pool.wait_ge(lx_loaded, 16 * b + 16)
                wait_drained(pool, segment, b, ("LO", t))
                pool.tensor_tensor(lx[:, t, :], lx[:, t, :], lg[:, t % 2, :], ALU.add).then_inc(lx_ready, 1)

            def unit(segment, b, u):
                kind, i = u
                if kind == "FC":
                    if segment != "tail" or i % 2 == 0:
                        square_low(pool, segment, b, i)
                elif kind == "ZT":
                    low_part(segment, b, i)
                elif kind == "LO":
                    add_x(segment, b, i)

            def iteration(segment, b, first=False, last=False):
                for s in range(SLOTS):
                    for u in slot_units(s, first, last):
                        unit(segment, b, u)
                    if not first:
                        if s == 2:
                            gather(b - 1, last)
                        if s == 5:
                            rstd3(b - 1)
                        if s == 20:
                            final(pool, b - 1, 0)
                    if s == 3:
                        save_rank(b)
                    if not last:
                        if s == 2:
                            rstd1(b + 1)
                        if s == 7:
                            rstd2(b + 1)
                        if s == 8:
                            norm_rows(segment, b + 1)
                        if 14 <= s < 14 + T:
                            scatter(segment, b + 1, 0, s - 14)
                        if 17 <= s < 17 + T:
                            scatter(segment, b + 1, 1, s - 17)
                if not first:
                    final(pool, b - 1, 1)

            rstd1(0)
            rstd2(0)
            norm_rows("start", 0)
            pool.wait_ge(low_made, KD)
            pool.memset(qbd[:, :, :, :], 0.0).then_inc(zeros_made, 1)
            for k in range(KD):
                low_part("start", -1, k)
            for r in range(2):
                for t in range(T):
                    scatter("start", 0, r, t)
            iteration("first", 0, first=True)
            with pool.Fori(1, B - 1) as b:
                iteration("loop", b)
            iteration("last", B - 1, last=True)
            gather(B - 1, True, in_tail=True)
            for half in range(2):
                rstd3(B - 1, half)
            for u in SEGMENTS["tail"]:
                unit("tail", B, u)
            final(pool, B - 1, 0)

        @block.scalar
        def _(act):
            act.dma_start(ln_cols[:, 0, :], ln_g.rearrange("(k p) -> p k", p=P), allow_slow_non_contiguous=True).then_inc(small_loaded, 16)
            act.dma_start(ln_cols[:, 1, :], ln_b.rearrange("(k p) -> p k", p=P), allow_slow_non_contiguous=True).then_inc(small_loaded, 16)
            act.dma_start(gamma_cols[:, 0, :], gamma_h.rearrange("(k p) -> p k", p=P), allow_slow_non_contiguous=True).then_inc(small_loaded, 16)
            act.wait_ge(c_loaded, 16)
            act.activation(silu[:, 1, :], silu[:, 0, :], ACT.Exp, scale=-1.0).then_inc(exp_c, 1)
            act.wait_ge(wqkv_loaded, 32)
            for k in range(KD):
                act.activation(wqkv[0][:, k, :], raw_wqkv[k], ACT.Copy).then_inc(high_made, 1)

            def drain(segment, b, unit):
                bank, before = bank_use(segment, b, unit)
                act.wait_ge(filled[bank], before + 1)
                return ps_unit[bank], drained[bank]

            def query(segment, b, unit):
                kind, i = unit
                ps, free = drain(segment, b, unit)
                if segment == "start":
                    act.wait_ge(zeros_made, 2)
                for h in range(2):
                    rows = slice(h * DH, (h + 1) * DH)
                    if kind == "Q":
                        src = ps[rows, :].rearrange("p (w q) -> p w q", q=W)
                        dst = qbd[rows, i % 2, :, h * W:(h + 1) * W]
                    else:
                        src = ps[rows, :].rearrange("p (a w q) -> p a w q", a=2, q=W)
                        dst = qbd_r[rows, 2 * i:2 * i + 2, :, h * W:(h + 1) * W]
                    ins = act.activation(dst, src, ACT.Copy, scale=-SCALE)
                ins.then_inc(free, 1)

            def unit(segment, b, u):
                kind, i = u
                if kind in ("Q", "NQ", "HQ"):
                    query(segment, b, u)
                elif kind in ("K", "NK"):
                    ps, free = drain(segment, b, u)
                    act.activation(kT[:, i % 2, :], ps[:, :], ACT.Copy).then_inc(free, 1)
                elif kind == "HK":
                    ps, free = drain(segment, b, u)
                    act.activation(kT_r[:, 2 * i:2 * i + 2, :], ps[:, :].rearrange("p (a n) -> p a n", a=2),
                                   ACT.Copy).then_inc(free, 1)
                elif kind == "ZT":
                    ps, free = drain(segment, b, u)
                    if segment == "start":
                        act.wait_ge(small_loaded, 80)
                    act.wait_ge(h1_ready, b + 2)
                    if segment == "loop":
                        act.wait_ge(h2_low, 2 * b)
                    act.activation(full[:, i, :], ps[:, :], ACT.Identity, bias=ln_cols[:, 1, i:i + 1],
                                   scale=ln_cols[:, 0, i:i + 1]).then_inc(free, 1)
                elif kind == "Z3":
                    ps, free = drain(segment, b, u)
                    n = b - 1
                    act.wait_ge(xT_low, 2 * B if segment == "tail" else 2 * b + 2)
                    if segment == "loop":
                        act.wait_ge(h1_ready, b + 2)
                    if segment == "tail":
                        act.wait_ge(h2_low, 2 * b - 2)
                    col = slice(n, n + 1) if isinstance(n, int) else bass.ds(n, 1)
                    k, _, cols = norm_tokens(segment, i)
                    act.activation(full[:, k, cols], ps[:, cols], ACT.Identity, bias=shift_b[:, k, col],
                                   scale=scale_b[:, k, col]).then_inc(free, 1)
                elif kind in ("WF", "WP"):
                    ps, _ = drain(segment, b, u)
                    act.activation(mlp_weight(0, u), ps[:, :], ACT.Copy).then_inc(high_made, 1)
                elif kind == "SR":
                    ps, free = drain(segment, b, u)
                    if i == 1 or segment != "start":
                        act.wait_ge(compared, 2 * b + 2 + i)
                    act.activation(score_row, ps[:, :], ACT.Copy).then_inc(free, 1)
                elif kind == "HT":
                    ps, _ = drain(segment, b, u)
                    for k in range(KD):
                        ins = act.activation(hT[0][:, i, k, :], ps[:, k * SEL:(k + 1) * SEL], ACT.Identity,
                                             scale=gamma_cols[:, 1, k:k + 1])
                    ins.then_inc(hT_high, 1)
                elif kind == "FC":
                    ps, free = drain(segment, b, u)
                    n = FT * (b - 1) + i
                    if i >= 2:
                        act.wait_ge(*low_made_of(segment, b, i - 2))
                    elif segment in ("last", "tail"):
                        act.wait_ge(hid_low, n - 1)
                    _, cols = chunk_tokens(segment, i)
                    act.activation(hid_relu[:, i % 2, cols], ps[:, cols], ACT.Relu).then_inc(free, 1)
                    wait_drained(act, segment, b, u)
                    if i >= 2 or segment == "tail" or segment == "last":
                        act.wait_ge(hid_used, n - 1)
                    act.activation(hid_parts[0][:, i % 2, cols], hid_relu[:, i % 2, cols],
                                   ACT.Square).then_inc(hid_high, 1)

            def negate_y(b, half, chunks):
                act.wait_ge(hid_used, FT * (b - 1) + chunks)
                act.wait_ge(out_stored, 32 * (b - 1) + 16)
                act.activation(spikes[:, half, :], ps_y[half][:, :], ACT.Copy, scale=-1.0).then_inc(y_negated, 1)

            def routed_weights(k):
                act.wait_ge(wr_loaded, 48)
                act.activation(wq_r[0][:, k, :], raw_wq[:, k, :], ACT.Copy).then_inc(high_made, 1)
                act.activation(wkv_r[0][:, k, :], raw_wkv[k], ACT.Copy).then_inc(high_made, 1)

            def exp_step(n, s):
                act.wait_ge(min_ready, n + 1)
                if isinstance(n, int) and n == 0:
                    act.wait_ge(zero_rows_stored, 16)
                ps = ps_scores[s % 2]
                for half, (lo, hi) in enumerate(score_columns(s)):
                    ins = act.activation(probs[:, s % 3, lo:hi], ps[:, lo:hi], ACT.Exp,
                                         bias=row_min[:, s % 3, half:half + 1], scale=-1.0,
                                         accum_out=row_sum[:, s % 3, half:half + 1])
                ins.then_inc(exp_ready, 1)

            def normalize(n, s):
                act.wait_ge(inv_ready, n + 1)
                for half, (lo, hi) in enumerate(score_columns(s)):
                    ins = act.activation(probs[:, s % 3, lo:hi], probs[:, s % 3, lo:hi], ACT.Identity,
                                         scale=row_inv[:, s % 3, half:half + 1])
                ins.then_inc(probs_ready, 1)

            def copy_pT(n, s):
                act.wait_ge(pT_ready, n + 1)
                if not (isinstance(n, int) and n == 0):
                    act.wait_ge(oT_ready, n)
                cols = 384 if s < LIGHT else 512
                act.activation(probsT[:, 0:cols], ps_pT[:, 0:cols], ACT.Copy).then_inc(pT_copied, 1)

            def iteration(segment, b, first=False, last=False):
                for s in range(SLOTS):
                    n = SLOTS * b + s
                    if first and s in (1, 2):
                        routed_weights(s - 1)
                    if not (first and s == 0):
                        copy_pT(n - 1, (s - 1) % SLOTS)
                    if not (last and s + 1 >= SLOTS):
                        normalize(n + 1, (s + 1) % SLOTS)
                    if not first and s == 17:
                        negate_y(b, 0, FT)
                        negate_y(b, 1, FT)
                    for u in slot_units(s, first, last):
                        unit(segment, b, u)
                    if not (last and s + 2 >= SLOTS):
                        exp_step(n + 2, (s + 2) % SLOTS)

            for u in SEGMENTS["start"]:
                unit("start", -1, u)
            exp_step(0, 0)
            exp_step(1, 1)
            normalize(0, 0)
            iteration("first", 0, first=True)
            with act.Fori(1, B - 1) as b:
                iteration("loop", b)
            iteration("last", B - 1, last=True)
            copy_pT(SLOTS * B - 1, SLOTS - 1)
            for u in SEGMENTS["tail"]:
                unit("tail", B, u)
                if u == ("FC", FT + 1):
                    negate_y(B, 0, FT)
            negate_y(B, 1, 2 * FT)

        @block.tensor
        def _(pe):
            def fill(segment, b, unit):
                bank, before = bank_use(segment, b, unit)
                if not (isinstance(before, int) and before == 0):
                    pe.wait_ge(drained[bank], before)
                return ps_unit[bank], filled[bank]

            def split_product(ps, w, w_cols, a, a_cols):
                n = 0
                for k in range(KD):
                    for wi, ai in ((0, 0), (0, 1), (1, 0)):
                        ins = pe.matmul(ps, w(wi, k, w_cols), a(ai, k, a_cols), start=(n == 0), stop=(n == 3 * KD - 1))
                        n += 1
                return ins

            def unit(segment, b, u):
                kind, i = u
                if kind == "YA":
                    project(segment, b, i)
                    return
                if segment == "first" and u in (("HV", 0), ("HV", 1)):
                    pe.wait_ge(low_made, LOW_PARTS)
                if segment == "first" and u == ("WF", 0):
                    pe.wait_ge(wmlp_loaded, 64)
                ps, full_bank = fill(segment, b, u)
                if kind in ("Q", "K", "NQ", "NK"):
                    if u == ("NQ", 0):
                        pe.wait_ge(xT_high, 2 * b + 4)
                        pe.wait_ge(xT_low, 2 * b + 4)
                    c0 = (0 if kind in ("Q", "NQ") else INNER) + i * P
                    ins = split_product(ps[:, :], lambda p, k, cc: wqkv[p][:, k, cc], slice(c0, c0 + P),
                                        lambda p, k, cc: xT[p][:, k, cc], slice(0, N))
                elif kind in ("V", "NV"):
                    ins = split_product(ps[:, :], lambda p, k, cc: xT[p][:, k, cc], slice(i * P, i * P + P),
                                        lambda p, k, cc: wqkv[p][:, k, cc], slice(2 * INNER, 3 * INNER))
                elif kind == "HT":
                    if i == 0:
                        pe.wait_ge(sorted_loaded, 32 * b + 32)
                    for k in range(KD):
                        for t in range(2):
                            ins = pe.transpose(ps[:, k * SEL + t * P:k * SEL + t * P + P],
                                               routed[:, i, t, k * P:k * P + P], ident[:, :])
                elif kind in ("HQ", "HK"):
                    r = 0 if kind == "HQ" else 1
                    if i == 0:
                        pe.wait_ge(hT_high, 2 * b + 1 + r)
                        if bank_use(segment, b, u)[0] != bank_use(segment, b, ("HT", r))[0]:
                            wait_drained(pe, segment, b, ("HT", r))
                    w = wq_r if kind == "HQ" else wkv_r
                    for j in range(2):
                        c0 = (2 * i + j) * P
                        ins = split_product(ps[:, j * SEL:(j + 1) * SEL], lambda p, k, cc: w[p][:, k, cc],
                                            slice(c0, c0 + P), lambda p, k, cc: hT[p][:, r, k, cc], slice(0, SEL))
                elif kind == "HV":
                    ins = split_product(ps[:, :], lambda p, k, cc: hT[p][:, 1, k, cc], slice(i * P, i * P + P),
                                        lambda p, k, cc: wkv_r[p][:, k, cc], slice(INNER, 2 * INNER))
                elif kind == "LO":
                    pe.wait_ge(oT_copied, SLOTS * b + LIGHT)
                    for p in range(PAIRS):
                        ins = pe.matmul(ps[:, 0:D], loT[:, p, i * P:(i + 1) * P], wo_light[:, p, :],
                                        start=(p == 0), stop=(p == PAIRS - 1))
                elif kind == "HO":
                    pe.wait_ge(oT_copied, SLOTS * b)
                    for p in range(PAIRS):
                        ins = pe.matmul(ps[:, 0:D], hoT[:, p, i * P:(i + 1) * P], wo_heavy[:, p, :],
                                        start=(p == 0), stop=(p == PAIRS - 1))
                elif kind == "ZT":
                    pe.wait_ge(z_ready, b + 2)
                    for t in range(T):
                        ins = pe.transpose(ps[:, t * P:(t + 1) * P], xa[:, t, i * P:(i + 1) * P], ident[:, :])
                elif kind == "Z3":
                    k, tiles, _ = norm_tokens(segment, i)
                    pe.wait_ge(z3_ready, b + (i // KD if segment == "tail" else 0))
                    for t in tiles:
                        ins = pe.transpose(ps[:, t * P:(t + 1) * P], gathered[:, t, k * P:(k + 1) * P], ident[:, :])
                elif kind == "WF":
                    k, g = divmod(i, 2)
                    for t in range(4):
                        ins = pe.transpose(ps[:, t * P:(t + 1) * P], raw_wfc[g][:, t, k * P:(k + 1) * P], ident[:, :])
                elif kind == "WP":
                    for a in range(2):
                        for dt in range(KD):
                            f = 2 * i + a
                            ins = pe.transpose(ps[:, a * D + dt * P:a * D + (dt + 1) * P],
                                               raw_wproj[dt][:, f * P:(f + 1) * P], ident[:, :])
                elif kind == "SR":
                    pe.wait_ge(score_ready, 2 * b + 3 + i)
                    for t in range(T):
                        ins = pe.transpose(ps[:, t * P:(t + 1) * P], score[:, i, t:t + 1].to_broadcast([P, P]),
                                           ident[:, :])
                elif kind == "RK":
                    pe.wait_ge(compared, 2 * b + 3 + i)
                    for t in range(T):
                        for j in range(T):
                            pe.matmul(ps[:, t:t + 1], greater[:, j, t * P:(t + 1) * P], ones_bf[:, 0:1],
                                      start=(j == 0), stop=False)
                        ins = pe.matmul(ps[:, t:t + 1], tie[:, t, :], ones_bf[:, 0:1], start=False, stop=True)
                elif kind == "FC":
                    if i == 0:
                        pe.wait_ge(h2_high, 2 * b)
                        pe.wait_ge(h2_low, 2 * b)
                    if i == FT:
                        pe.wait_ge(h2_high, 2 * b + KD)
                        pe.wait_ge(h2_low, 2 * b + KD)
                    f, cols = chunk_tokens(segment, i)
                    ins = split_product(ps[:, cols], lambda p, k, cc: wfcT[p][:, k, cc], slice(f * P, f * P + P),
                                        lambda p, k, cc: h2T[p][:, k, cc], cols)
                ins.then_inc(full_bank, 1)

            def project(segment, b, i):
                n = FT * (b - 1) + i
                f, tokens = chunk_tokens(segment, i)
                if i == 0:
                    pe.wait_ge(y_free, 2 * b)
                pe.wait_ge(hid_high, n + 1)
                pe.wait_ge(*low_made_of(segment, b, i))
                for t in range(tokens.start // P, tokens.stop // P):
                    for j, (hi, wi) in enumerate(((0, 0), (0, 1), (1, 0))):
                        ins = pe.matmul(ps_y[t // 2][:, (t % 2) * D:(t % 2 + 1) * D],
                                        hid_parts[hi][:, i % 2, t * P:(t + 1) * P], wprojT[wi][:, f, :],
                                        start=(f == 0 and t % 2 == 0 and j == 0),
                                        stop=(f == FT - 1 and t % 2 == 1 and j == 2))
                ins.then_inc(hid_used, 1)

            def scores(segment, b, n, s):
                if not (isinstance(n, int) and n < 2):
                    pe.wait_ge(exp_ready, n - 1)
                ps = ps_scores[s % 2]
                columns = score_columns(s)
                if s < LIGHT:
                    p, m = divmod(s, T)
                    if s == 0:
                        wait_drained(pe, segment, b, ("NQ", 0), ("NK", 0))
                    if m == 0 and p > 1:
                        wait_drained(pe, segment, b, ("Q", p), ("K", p))
                    for half, window in enumerate((2 * m + 1, 2 * m)):
                        lo, hi = columns[half]
                        k0 = m * P if half == 0 else (m + 1) * P - (hi - lo)
                        ins = pe.matmul(ps[:, lo:hi], qbd[:, p % 2, window, :], kT[:, p % 2, k0:k0 + hi - lo],
                                        start=True, stop=True)
                else:
                    p, j = divmod(s - LIGHT, SEL // P)
                    if j == 0 and p % 2 == 0:
                        wait_drained(pe, segment, b, ("HQ", p // 2), ("HK", p // 2))
                    for half, (lo, hi) in enumerate(columns):
                        ins = pe.matmul(ps[:, lo:hi], qbd_r[:, p, 2 * j + half, :], kT_r[:, p, :],
                                        start=True, stop=True)
                ins.then_inc(scores_ready, 1)

            def turn(n, s):
                pe.wait_ge(probs_ready, n + 1)
                if not (isinstance(n, int) and n == 0):
                    pe.wait_ge(pT_copied, n)
                blocks = [(i, i) for i in range(3)] if s < LIGHT else [(0, 0), (1, 2), (2, 1), (3, 3)]
                for src, dst in blocks:
                    ins = pe.transpose(ps_pT[:, dst * P:(dst + 1) * P], probs[:, s % 3, src * P:(src + 1) * P],
                                       ident[:, :])
                ins.then_inc(pT_ready, 1)

            def attend(segment, b, n, s):
                pe.wait_ge(pT_copied, n + 1)
                if not (isinstance(n, int) and n == 0):
                    pe.wait_ge(oT_copied, n)

                if s < LIGHT:
                    p, m = divmod(s, T)
                    cols = slice(p * P, (p + 1) * P)
                    if p == 0:
                        if m == 2:
                            wait_drained(pe, segment, b, ("V", 3))
                    even, odd = ps_oT[:, 0:P], ps_oT[:, P:2 * P]
                    if m > 0:
                        ins = pe.matmul(even, v[W:P, m - 1, cols], probsT[W:P, P:2 * P], start=True, stop=False)
                        if m < T - 1:
                            ins.then_inc(outer_done, 1)
                    pe.matmul(even, v[:, m, cols], probsT[:, 2 * P:3 * P], start=(m == 0), stop=True)
                    ins = pe.matmul(odd, v[:, m, cols], probsT[:, 0:P], start=True, stop=(m == T - 1))
                    if m < T - 1:
                        if m > 0:
                            pe.wait_ge(outer_done, (T - 2) * (PAIRS * b + p) + m)
                        ins = pe.matmul(odd, v[0:W, m + 1, cols], probsT[0:W, P:2 * P], start=False, stop=True)
                else:
                    p, _ = divmod(s - LIGHT, SEL // P)
                    if s == LIGHT:
                        wait_drained(pe, segment, b, ("HV", 0), ("HV", 1))
                    for t in range(2):
                        ins = pe.matmul(ps_oT[:, 0:2 * P], v_r[:, t, p * P:(p + 1) * P],
                                        probsT[:, t * 2 * P:(t + 1) * 2 * P], start=(t == 0), stop=(t == 1))
                ins.then_inc(oT_ready, 1)

            def iteration(segment, b, first=False, last=False):
                for s in range(SLOTS):
                    n = SLOTS * b + s
                    if not (last and s + 2 >= SLOTS):
                        scores(segment, b, n + 2, (s + 2) % SLOTS)
                    for u in slot_units(s, first, last):
                        unit(segment, b, u)
                    turn(n, s)
                    if not (first and s == 0):
                        attend(segment, b, n - 1, (s - 1) % SLOTS)
                if not last:
                    wait_drained(pe, segment, b, *PROJECTED_AHEAD)

            pe.wait_ge(consts_made, 6)
            pe.wait_ge(silu_ready, 1)
            ps, full_bank = fill("setup", 0, ("SC", 0))
            for k in range(KD):
                ins = pe.transpose(ps[:, k * B:(k + 1) * B], silu[:, 2, k * P:(k + 1) * P], ident[0:B, 0:B])
            ins.then_inc(full_bank, 1)
            wait_drained(pe, "setup", 0, ("SC", 0))
            pe.wait_ge(wmod_norm_loaded, 32)
            ps, full_bank = fill("setup", 0, ("MB", 0))
            for k in range(KD):
                ins = pe.matmul(ps[:, :], silu_first[:, k, :], raw_wmod[k][:, 0:512], start=(k == 0), stop=(k == KD - 1))
            ins.then_inc(full_bank, 1)
            pe.wait_ge(wmod_rest_loaded, 32)
            ps, full_bank = fill("setup", 0, ("MC", 0))
            for q in range(4):
                for k in range(KD):
                    ins = pe.matmul(ps[:, q * B:(q + 1) * B], raw_wmod[k][:, 3 * D + q * P:3 * D + (q + 1) * P],
                                    siluT[:, k, :], start=(k == 0), stop=(k == KD - 1))
            ins.then_inc(full_bank, 1)
            for i in range(3):
                ps, full_bank = fill("setup", 0, ("MR", i))
                for k in range(KD):
                    ins = pe.matmul(ps[0:B, :], siluT[:, k, :], raw_wmod[k][:, i * 512:(i + 1) * 512],
                                    start=(k == 0), stop=(k == KD - 1))
                ins.then_inc(full_bank, 1)

            for u in SEGMENTS["start"]:
                if u == ("NQ", 0):
                    pe.wait_ge(low_made, KD)
                    pe.wait_ge(wo_loaded, 32)
                unit("start", -1, u)
            scores("start", -1, 0, 0)
            scores("start", -1, 1, 1)
            wait_drained(pe, "start", -1, *PROJECTED_AHEAD)
            iteration("first", 0, first=True)
            with pe.Fori(1, B - 1) as b:
                iteration("loop", b)
            iteration("last", B - 1, last=True)
            attend("tail", B, SLOTS * B - 1, SLOTS - 1)
            for u in SEGMENTS["tail"]:
                unit("tail", B, u)

        @block.vector
        def _(dve):
            def drain(segment, b, unit):
                bank, before = bank_use(segment, b, unit)
                dve.wait_ge(filled[bank], before + 1)
                return ps_unit[bank], drained[bank]

            def stats1(n):
                dve.wait_ge(x_loaded, 16 * n + 16)
                for t in range(T):
                    ins = dve.bn_stats(bn6[:, 0, t, :], xa[:, t, :])
                ins.then_inc(ln_chain, 1)
                dve.wait_ge(ln_chain, 3 * n + 1)
                seal_waits(dve)
                for t in range(T):
                    ins = dve.bn_aggr(mv[:, 0, t, :], bn6[:, 0, t, :])
                ins.then_inc(mv1_ready, 1)

            def center(n):
                if isinstance(n, int) and n == 0:
                    wait_drained(dve, "setup", 0, ("MB", 0))
                else:
                    dve.wait_ge(mod_a_loaded, 16 * n)
                dve.wait_ge(mv1_ready, n + 1)
                for t in range(T):
                    ins = dve.scalar_tensor_tensor(out=xa[:, t, :], in0=xa[:, t, :], scalar=mv[:, 0, t, 0:1],
                                                   in1=mod_a[:, 0, :], op0=ALU.subtract, op1=ALU.mult)
                ins.then_inc(ln_chain, 1)

            def modulate(n):
                dve.wait_ge(ln_chain, 3 * n + 2)
                dve.wait_ge(rstd1_ready, n + 1)
                for t in range(T):
                    ins = dve.scalar_tensor_tensor(out=h1[:, t, :], in0=xa[:, t, :], scalar=rstd[:, 0, t:t + 1],
                                                   in1=mod_a[:, 1, :], op0=ALU.mult, op1=ALU.add)
                ins.then_inc(h1_ready, 1)

            def stats2(n):
                dve.wait_ge(h1_ready, n + 1)
                for t in range(T):
                    ins = dve.bn_stats(bn6[:, 1, t, :], h1[:, t, :])
                ins.then_inc(ln_chain, 1)
                dve.wait_ge(ln_chain, 3 * n + 3)
                seal_waits(dve)
                for t in range(T):
                    ins = dve.bn_aggr(mv[:, 1, t, :], bn6[:, 1, t, :])
                ins.then_inc(mv2_ready, 1)

            def router_scores(n, r):
                if isinstance(n, int) and n == 0 and r == 0:
                    dve.wait_ge(small_loaded, 80)
                if r == 1:
                    dve.wait_ge(score_ready, 2 * n + 1)
                for t in range(T):
                    ins = dve.tensor_tensor_reduce(products[:, t, :], h1[:, t, :], router[:, r, :], 1.0, 0.0,
                                                   ALU.mult, ALU.add, score[:, r, t:t + 1])
                ins.then_inc(score_ready, 1)

            def second_norm(n):
                dve.wait_ge(mv2_ready, n + 1)
                dve.wait_ge(rstd2_ready, n + 1)
                for t in range(T):
                    ins = dve.tensor_scalar(xa[:, t, :], h1[:, t, :], mv[:, 1, t, 0:1], rstd[:, 1, t:t + 1],
                                            ALU.subtract, ALU.mult)
                ins.then_inc(z_ready, 1)

            def compare(segment, n, r):
                wait_drained(dve, segment, n - 1, ("SR", r))
                if r == 1:
                    wait_drained(dve, segment, n - 1, ("RK", 0))
                dve.wait_ge(score_ready, 2 * n + r + 1)
                for j in range(T):
                    s = score[:, r, j:j + 1]
                    e = (j + 1) * P
                    dve.tensor_scalar(greater[:, j, 0:e], score_row[:, 0:e], s, None, ALU.is_gt)
                    if j < T - 1:
                        dve.tensor_scalar(greater[:, j, e:N], score_row[:, e:N], s, None, ALU.is_ge)
                    ins = dve.scalar_tensor_tensor(out=tie[:, j, :], in0=score_row[:, j * P:e], scalar=s,
                                                   in1=later[:, :], op0=ALU.is_equal, op1=ALU.mult)
                ins.then_inc(compared, 1)

            def high_part(segment, b, unit):
                kind, i = unit
                n, highs, parts = (b + 1, xT_high, xT) if kind == "ZT" else (b - 1, h2_high, h2T)
                k, _, cols = norm_tokens(segment, i)
                wait_drained(dve, segment, b, unit)
                dve.tensor_copy(parts[0][:, k, cols], full[:, k, cols]).then_inc(highs, 1)
                if kind == "Z3":
                    dve.wait_ge(highs, KD * n + i + 1)
                    dve.tensor_tensor(parts[1][:, k, cols], full[:, k, cols], parts[0][:, k, cols].bitcast(F32),
                                      ALU.subtract).then_inc(h2_low, 1)

            def add_rows(n, half=None):
                dve.wait_ge(lx_ready, T * n + T)
                if half is None:
                    dve.wait_ge(rows_gathered, 64 * n + 64)
                elif half == 0:
                    dve.wait_ge(rows_gathered, 64 * n + 32)
                else:
                    dve.wait_ge(tail_gathered, 32)
                dve.wait_ge(final_ready, 2 * n + 1)
                ts = slice(half_tiles(half).start, half_tiles(half).stop)
                dve.tensor_tensor(x2[:, ts, :], lx[:, ts, :], gathered[:, ts, :], ALU.add).then_inc(x2_ready, 1)

            def stats3(n, half=None):
                count = n + 1 + (half or 0)
                dve.wait_ge(x2_ready, count)
                for t in half_tiles(half):
                    ins = dve.bn_stats(bn6[:, 2, t, :], x2[:, t, :])
                ins.then_inc(d_chain, 1)
                dve.wait_ge(d_chain, count)
                seal_waits(dve)
                for t in half_tiles(half):
                    ins = dve.bn_aggr(mv[:, 2, t, :], bn6[:, 2, t, :])
                ins.then_inc(mv3_ready, 1)

            def third_norm(n, half=None):
                count = n + 1 + (half or 0)
                dve.wait_ge(mv3_ready, count)
                dve.wait_ge(rstd3_ready, count)
                for t in half_tiles(half):
                    ins = dve.tensor_scalar(gathered[:, t, :], x2[:, t, :], mv[:, 2, t, 0:1], rstd[:, 2, t:t + 1],
                                            ALU.subtract, ALU.mult)
                ins.then_inc(z3_ready, 1)

            def neuron(segment, b, half, step):
                n = b - 1
                base = 24 * n + 12 * half

                def after(k):
                    dve.wait_ge(lif_chain, base + k)

                yh = ps_y[half][:, :]
                spk = spikes[:, half, :]
                if step == 1:
                    dve.wait_ge(y_negated, 2 * n + half + 1)
                    if half == 1:
                        after(0)
                    dve.scalar_tensor_tensor(out=drive, in0=spk, scalar=0.9, in1=yh, op0=ALU.mult,
                                             op1=ALU.subtract).then_inc(lif_chain, 1)
                    after(1)
                    dve.scalar_tensor_tensor(out=neg_mem, in0=spk, scalar=-1.0, in1=drive,
                                             op0=ALU.is_lt, op1=ALU.add).then_inc(lif_chain, 1)
                    after(2)
                    dve.tensor_scalar(spk, spk, -1.0, None, ALU.is_lt).then_inc(lif_chain, 1)
                    after(3)
                    dve.scalar_tensor_tensor(out=spk, in0=neg_mem, scalar=-1.0, in1=spk, op0=ALU.is_lt,
                                             op1=ALU.add).then_inc(lif_chain, 1)
                    return
                k = 4 + 3 * (step - 2)
                dve.scalar_tensor_tensor(out=drive, in0=neg_mem, scalar=0.9, in1=yh, op0=ALU.mult,
                                         op1=ALU.subtract).then_inc(lif_chain, 1)
                after(k + 1)
                dve.scalar_tensor_tensor(out=neg_mem, in0=neg_mem, scalar=-1.0, in1=drive,
                                         op0=ALU.is_lt, op1=ALU.add).then_inc(lif_chain, 1)
                after(k + 2)
                last_step = step == STEPS - 1
                dve.scalar_tensor_tensor(out=spk, in0=neg_mem, scalar=-1.0, in1=spk, op0=ALU.is_lt,
                                         op1=ALU.add).then_inc(y_free if last_step else lif_chain, 1)

            def minimum(n, s):
                dve.wait_ge(scores_ready, n + 1)
                ps = ps_scores[s % 2]
                columns = score_columns(s)
                if columns[0][1] == columns[1][0] and columns[0][1] * 2 == columns[1][1]:
                    end = columns[1][1]
                    dve.tensor_reduce(row_min[:, s % 3, :], ps[:, 0:end].rearrange("p (a n) -> p a n", a=2), AX.X,
                                      ALU.min).then_inc(min_ready, 1)
                else:
                    for half, (lo, hi) in enumerate(columns):
                        ins = dve.tensor_reduce(row_min[:, s % 3, half:half + 1], ps[:, lo:hi], AX.X, ALU.min)
                    ins.then_inc(min_ready, 1)

            def invert(n, s):
                dve.wait_ge(exp_ready, n + 1)
                dve.reciprocal(row_inv[:, s % 3, :], row_sum[:, s % 3, :]).then_inc(inv_ready, 1)

            def copy_out(n, s):
                dve.wait_ge(oT_ready, n + 1)
                if s < LIGHT:
                    p, m = divmod(s, T)
                    dst = loT
                else:
                    p, m = divmod(s - LIGHT, SEL // P)
                    dst = hoT
                for h in range(2):
                    rows = slice(h * DH, (h + 1) * DH)
                    ins = dve.tensor_copy(
                        dst[rows, p, m * P:(m + 1) * P].rearrange("p (w q) -> p w q", w=2),
                        ps_oT[rows, 0:2 * P].rearrange("p (w q) -> p w q", w=2)[:, :, h * W:(h + 1) * W])
                ins.then_inc(oT_copied, 1)

            def unit(segment, b, u):
                kind, i = u
                if kind in ("WF", "WP"):
                    ps, free = drain(segment, b, u)
                    dve.wait_ge(high_made, WF_HIGH + FIRST_WEIGHTS.index(u) + 1)
                    dve.tensor_tensor(mlp_weight(1, u), ps[:, :], mlp_weight(0, u).bitcast(F32),
                                      ALU.subtract).then_inc(free, 1)
                elif kind in ("V", "NV", "HV"):
                    if segment == "start":
                        dve.wait_ge(mod_stored, 32)
                    ps, free = drain(segment, b, u)
                    dve.tensor_copy(v_r[:, i, :] if kind == "HV" else v[:, i, :], ps[:, :]).then_inc(free, 1)
                elif kind == "HT":
                    ps, free = drain(segment, b, u)
                    dve.wait_ge(hT_high, 2 * b + i + 1)
                    for k in range(KD):
                        ins = dve.scalar_tensor_tensor(
                            out=hT[1][:, i, k, :], in0=ps[:, k * SEL:(k + 1) * SEL], scalar=gamma_cols[:, 1, k:k + 1],
                            in1=hT[0][:, i, k, :].bitcast(F32), op0=ALU.mult, op1=ALU.subtract)
                    ins.then_inc(free, 1)
                elif kind == "RK":
                    ps, free = drain(segment, b, u)
                    if segment != "start":
                        dve.wait_ge(rank_saved, b + 1)
                    dve.tensor_copy(rank[:, i, :], ps[:, 0:T]).then_inc(free, 1)
                elif kind == "LO":
                    ps, free = drain(segment, b, u)
                    dve.wait_ge(gate_a_loaded, 16 * b + 16)
                    if i >= 2:
                        dve.wait_ge(lx_ready, T * b + i - 1)
                    dve.tensor_tensor(lg[:, i % 2, :], ps[:, 0:D], gate_a[:, :], ALU.mult).then_inc(free, 1)
                elif kind == "HO":
                    ps, free = drain(segment, b, u)
                    dve.tensor_tensor(ho[:, i, :], ps[:, 0:D], gate_a[:, :], ALU.mult).then_inc(free, 1)
                elif kind in ("ZT", "Z3"):
                    high_part(segment, b, u)

            def routed_weights(k):
                dve.wait_ge(high_made, KD + 1 + 2 * k)
                dve.tensor_tensor(wq_r[1][:, k, :], raw_wq[:, k, :], wq_r[0][:, k, :].bitcast(F32),
                                  ALU.subtract).then_inc(low_made, 1)
                dve.wait_ge(high_made, KD + 2 + 2 * k)
                dve.tensor_tensor(wkv_r[1][:, k, :], raw_wkv[k], wkv_r[0][:, k, :].bitcast(F32),
                                  ALU.subtract).then_inc(low_made, 1)

            NEURON = {17: [(0, 1)], 18: [(0, 2), (0, 3)], 19: [(0, 4), (1, 1)], 20: [(1, 2)], 21: [(1, 3)], 22: [(1, 4)]}

            def stages(segment, b, s, first, last):
                if not first:
                    if s == 5:
                        add_rows(b - 1)
                        stats3(b - 1)
                    if s == 6:
                        third_norm(b - 1)
                    for half, step in NEURON.get(s, []):
                        neuron(segment, b, half, step)
                if not last:
                    if s == 3:
                        center(b + 1)
                    if s == 4:
                        modulate(b + 1)
                    if s == 8:
                        router_scores(b + 1, 0)
                    if s == 9:
                        router_scores(b + 1, 1)
                    if s == 10:
                        second_norm(b + 1)
                    if s == 11:
                        compare(segment, b + 1, 0)
                    if s == 14:
                        compare(segment, b + 1, 1)

            def iteration(segment, b, first=False, last=False):
                for s in range(SLOTS):
                    n = SLOTS * b + s
                    if first and s in (2, 3):
                        routed_weights(s - 2)
                    if not (first and s < 2):
                        copy_out(n - 2, (s - 2) % SLOTS)
                    if not (last and s + 1 >= SLOTS):
                        invert(n + 1, (s + 1) % SLOTS)
                    if not (last and s + 2 >= SLOTS):
                        minimum(n + 2, (s + 2) % SLOTS)
                    if not last and s == 7:
                        stats2(b + 1)
                    for u in slot_units(s, first, last):
                        unit(segment, b, u)
                        if not last and u == (("V", 3) if first else ("HO", 0)):
                            stats1(b + 1)
                    stages(segment, b, s, first, last)

            step = [0]

            def link(ins):
                step[0] += 1
                ins.then_inc(setup_chain, 1)
                dve.wait_ge(setup_chain, step[0])

            dve.wait_ge(exp_c, 1)
            link(dve.tensor_scalar(silu[:, 1, :], silu[:, 1, :], 1.0, None, ALU.add))
            link(dve.reciprocal(silu[:, 1, :], silu[:, 1, :]))
            dve.tensor_tensor(silu[:, 2, :], silu[:, 0, :], silu[:, 1, :], ALU.mult).then_inc(silu_ready, 1)
            dve.memset(marks[:, 1:2], 0.0).then_inc(y_free, 2)
            dve.memset(marks[:, 2:3], 0.0).then_inc(out_stored, 16)
            ps, free = drain("setup", 0, ("SC", 0))
            columns = ps[:, 0:KD * B].rearrange("p (k b) -> p k b", k=KD)
            dve.tensor_copy(silu_first, columns[:, :, 0:1].to_broadcast([P, KD, P]))
            dve.tensor_copy(siluT[:, :, :], columns).then_inc(free, 1)
            stats1(0)
            ps, free = drain("setup", 0, ("MB", 0))
            dve.tensor_copy(mod_a[:, 1, :], ps[:, 0:D])
            dve.tensor_scalar(mod_a[:, 0, :], ps[:, D:2 * D], 1.0, None, ALU.add).then_inc(free, 1)
            center(0)
            modulate(0)
            stats2(0)
            router_scores(0, 0)
            ps, free = drain("setup", 0, ("MC", 0))
            cols = ps[:, 0:4 * B].rearrange("p (q b) -> p q b", q=4)
            dve.tensor_copy(shift_b[:, :, :], cols[:, 0:KD, :])
            dve.tensor_scalar(scale_b[:, :, :], cols[:, KD:2 * KD, :], 1.0, None, ALU.add).then_inc(free, 1)
            second_norm(0)
            for k in range(KD):
                dve.wait_ge(high_made, k + 1)
                dve.tensor_tensor(wqkv[1][:, k, :], raw_wqkv[k], wqkv[0][:, k, :].bitcast(F32),
                                  ALU.subtract).then_inc(low_made, 1)
            router_scores(0, 1)
            ps, free = drain("setup", 0, ("MR", 0))
            dve.tensor_copy(mod_norm[:, D:2 * D], ps[0:B, 0:D])
            dve.tensor_scalar(mod_norm[:, 0:D], ps[0:B, D:2 * D], 1.0, None, ALU.add).then_inc(free, 1)
            ps, free = drain("setup", 0, ("MR", 1))
            dve.tensor_copy(gates[:, 0:D], ps[0:B, 0:D]).then_inc(free, 1)
            ps, free = drain("setup", 0, ("MR", 2))
            dve.tensor_copy(gates[:, D:2 * D], ps[0:B, D:2 * D]).then_inc(free, 1)
            high_part("start", -1, ("ZT", 0))
            high_part("start", -1, ("ZT", 1))
            wait_drained(dve, "setup", 0, ("MR", 1), ("MR", 2))
            link(dve.scalar_tensor_tensor(out=gates_abs, in0=gates, scalar=-1.0, in1=gates, op0=ALU.mult, op1=ALU.max))
            link(dve.tensor_scalar(gates_abs, gates_abs, 0.25, None, ALU.max))
            link(dve.tensor_scalar(gates_sign, gates, 0.0, 2.0, ALU.is_ge, ALU.mult))
            link(dve.scalar_tensor_tensor(out=mod_gate, in0=gates_sign, scalar=-1.0, in1=gates_abs,
                                          op0=ALU.add, op1=ALU.mult))
            dve.tensor_scalar(mod_gate[:, D:2 * D], mod_gate[:, D:2 * D], 1.0 / STEPS, None,
                              ALU.mult).then_inc(mod_ready, 1)
            dve.tensor_scalar(gamma_cols[:, 1, :], gamma_cols[:, 0, :], float(D) ** 0.5, None,
                              ALU.mult).then_inc(low_made, 1)
            compare("start", 0, 0)
            unit("start", -1, ("RK", 0))
            unit("start", -1, ("NV", 0))
            unit("start", -1, ("NV", 1))
            compare("start", 0, 1)
            unit("start", -1, ("NV", 2))
            unit("start", -1, ("RK", 1))
            minimum(0, 0)
            minimum(1, 1)
            invert(0, 0)
            iteration("first", 0, first=True)
            with dve.Fori(1, B - 1) as b:
                iteration("loop", b)
            iteration("last", B - 1, last=True)
            copy_out(SLOTS * B - 2, SLOTS - 2)
            copy_out(SLOTS * B - 1, SLOTS - 1)
            for t in range(2):
                unit("tail", B, ("HO", t))
            for half in range(2):
                add_rows(B - 1, half)
                stats3(B - 1, half)
            for half in range(2):
                third_norm(B - 1, half)
            for i in range(KD):
                high_part("tail", B, ("Z3", i))
            for i in range(1, FT, 2):
                square_low(dve, "tail", B, i)
                if i == 1:
                    for j in range(KD, 2 * KD):
                        high_part("tail", B, ("Z3", j))
            for s in range(1, STEPS):
                square_low(dve, "tail", B, FT + 2 * s - 1)
                neuron("tail", B, 0, s)
            for s in range(1, STEPS):
                neuron("tail", B, 1, s)
            dve.wait_ge(final_ready, 2 * B)
            final(dve, B - 1, 1)


_INS = ["L0_attn_x", "L0_attn_gamma_h", "L0_attn_wq_h", "L0_attn_wkv_h", "L0_attn_wo_h", "L0_attn_ln_g",
        "L0_attn_ln_b", "L0_attn_wqkv_l", "L0_attn_wo_l", "L0_attn_rt_q", "L0_attn_rt_kv", "L0_ffn_W_fc",
        "L0_ffn_W_proj", "L0_c", "L0_wmod"]


def kernel(**inputs):
    import numpy as _np
    import concourse.bacc as _bacc
    from concourse import mybir as _mybir
    from concourse.bass_utils import run_bass_kernel_spmd as _run

    nc = _bacc.Bacc("TRN2", target_bir_lowering=False, num_devices=1)
    arrays, args = {}, []
    for name in _INS:
        a = _np.ascontiguousarray(inputs[name])
        arrays[f"in_{name}"] = a
        args.append(nc.dram_tensor(f"in_{name}", a.shape, _mybir.dt.from_np(a.dtype), kind="ExternalInput").ap())
    args.append(nc.dram_tensor("out_x", (B, N, D), F32, kind="ExternalOutput").ap())
    adaln_block_kernel(nc, *args)
    return _run(nc, [arrays], core_ids=[0]).results[0]["out_x"]
```
